# Optimizing a Trainium2 kernel written in Bass

```python
import numpy as np
import jax
import jax.numpy as jnp

def _softmax(x, axis=-1):
    return jax.nn.softmax(x, axis=axis)

def _gelu(x):
    return jax.nn.gelu(x, approximate=True)

def _silu(x):
    return jax.nn.silu(x)

def _sigmoid(x):
    return jax.nn.sigmoid(x)

def _layernorm(x, axis=-1, eps=1e-05):
    m = jnp.mean(x, axis=axis, keepdims=True)
    v = jnp.var(x, axis=axis, keepdims=True)
    return (x - m) / jnp.sqrt(v + eps)

def _scatter_add(tgt, idx, src, axis=0):
    return tgt.at[idx].add(src)

def _segment_sum(src, seg, n):
    return jax.ops.segment_sum(src, seg, n)
kernel_name = 'mk_gnn_preln_d4_gnn_r32_a7e525'

def setup_inputs(seed: int=0):
    np.random.seed(seed)
    _w = jnp.asarray

    def _rec_inputs():
        import jax
        import jax.numpy as jnp
        _gk = jax.random.key(seed)
        x = -0.000202 + 1 * jax.random.normal(jax.random.fold_in(_gk, 1), (3125, 64), jnp.float32)
        _s = jax.random.randint(jax.random.fold_in(_gk, 2), (50000,), 0, 3125, jnp.int32)
        _d = jax.random.randint(jax.random.fold_in(_gk, 3), (50000,), 0, 3125, jnp.int32)
        _loop = jnp.arange(3125, dtype=jnp.int32)
        src = jnp.concatenate([_s, _d, _loop])
        dst = jnp.concatenate([_d, _s, _loop])
        _o = jnp.argsort(dst, stable=True)
        src = src[_o]
        dst = dst[_o]
        edge_attr_16 = 0.000196303 + 1.00016 * jax.random.normal(jax.random.fold_in(_gk, 11), (103125, 16), jnp.float32)
        edge_weight1 = jax.random.uniform(jax.random.fold_in(_gk, 13), (103125, 1), jnp.float32, 0.0, 0.999999)
        return (x, src, dst, edge_attr_16, edge_weight1)
    x, src, dst, edge_attr_16, edge_weight1 = _rec_inputs()

    def _L0_gnn_setup():
        import jax, jax.numpy as jnp
        import numpy as np
        N_NODES = 3125
        N_EDGES = 50000
        D_IN = 64
        D_OUT = 64

        def _gcn_block(x, edge_index, edge_w, W, b, gamma, beta):
            n = x.shape[0]
            xw = x @ W
            loop = jnp.arange(n, dtype=edge_index.dtype)
            src = jnp.concatenate([edge_index[0], loop])
            dst = jnp.concatenate([edge_index[1], loop])
            w = jnp.concatenate([edge_w, jnp.ones((n,), dtype=x.dtype)])
            deg = jax.ops.segment_sum(w, dst, num_segments=n)
            dinv = jnp.where(deg > 0, jax.lax.rsqrt(deg), 0.0)
            norm = dinv[src] * w * dinv[dst]
            msg = xw[src] * norm[:, None]
            agg = jax.ops.segment_sum(msg, dst, num_segments=n)
            h = agg + b
            mu = jnp.mean(h, axis=-1, keepdims=True)
            var = jnp.mean(jnp.square(h - mu), axis=-1, keepdims=True)
            hn = (h - mu) * jax.lax.rsqrt(var + 1e-05) * gamma + beta
            return jax.nn.gelu(hn, approximate=False)
        key = jax.random.key(seed)
        ks = jax.random.split(key, 5)
        x = jax.random.normal(ks[0], (N_NODES, D_IN), dtype=jnp.float32)
        edge_index = jax.random.randint(ks[1], (2, N_EDGES), 0, N_NODES, dtype=jnp.int64)
        edge_attr = jax.random.uniform(ks[2], (N_EDGES, 1), dtype=jnp.float32)
        W = jax.random.normal(ks[3], (D_IN, D_OUT), dtype=jnp.float32) * (1.0 / np.sqrt(D_IN))
        b = jnp.zeros((D_OUT,), dtype=jnp.float32)
        gamma = jnp.ones((D_OUT,), dtype=jnp.float32)
        beta = jnp.zeros((D_OUT,), dtype=jnp.float32)
        return {'x': x, 'edge_index': edge_index, 'edge_attr': edge_attr, 'W': W, 'b': b, 'gamma': gamma, 'beta': beta}
    _L0_gnn_all = _L0_gnn_setup()
    _L0_gnn_in = {k: v for k, v in _L0_gnn_all.items() if k in ('W', 'b', 'gamma', 'beta')}
    del _L0_gnn_all

    def _L1_gnn_setup():
        import jax, jax.numpy as jnp
        import numpy as np
        N_NODES = 3125
        N_EDGES = 50000
        IN_DIM = 64
        OUT_DIM = 64

        def _gcn_conv(x, edge_index, W, b):
            n = x.shape[0]
            loop = jnp.arange(n, dtype=edge_index.dtype)
            src = jnp.concatenate([edge_index[0], loop])
            dst = jnp.concatenate([edge_index[1], loop])
            deg = jax.ops.segment_sum(jnp.ones_like(src, dtype=x.dtype), dst, num_segments=n)
            dinv = jax.lax.rsqrt(jnp.maximum(deg, 1.0))
            norm = dinv[src] * dinv[dst]
            h = x @ W
            msg = h[src] * norm[:, None]
            out = jax.ops.segment_sum(msg, dst, num_segments=n)
            return out + b
        key = jax.random.key(seed)
        k1, k2, k3, k4, k5, k6 = jax.random.split(key, 6)
        x = jax.random.normal(k1, (N_NODES, IN_DIM), dtype=jnp.float32)
        edge_index = jax.random.randint(k2, (2, N_EDGES), 0, N_NODES, dtype=jnp.int64)
        s = 1.0 / np.sqrt(IN_DIM)
        W = jax.random.uniform(k3, (IN_DIM, OUT_DIM), minval=-s, maxval=s, dtype=jnp.float32)
        b = jax.random.uniform(k4, (OUT_DIM,), minval=-s, maxval=s, dtype=jnp.float32)
        W_lin = jax.random.uniform(k5, (IN_DIM, OUT_DIM), minval=-s, maxval=s, dtype=jnp.float32)
        b_lin = jax.random.uniform(k6, (OUT_DIM,), minval=-s, maxval=s, dtype=jnp.float32)
        return {'x': x, 'edge_index': edge_index, 'W': W, 'b': b, 'W_lin': W_lin, 'b_lin': b_lin}
    _L1_gnn_all = _L1_gnn_setup()
    _L1_gnn_in = {k: v for k, v in _L1_gnn_all.items() if k in ('W', 'b', 'W_lin', 'b_lin')}
    del _L1_gnn_all

    def _L2_gnn_setup():
        import jax, jax.numpy as jnp
        import numpy as np
        N_NODES = 3125
        N_EDGES = 50000
        D_IN = 64
        D_OUT = 64
        EDGE_DIM = 16
        key = jax.random.key(seed)
        ks = jax.random.split(key, 6)
        x = jax.random.normal(ks[0], (N_NODES, D_IN), dtype=jnp.float32)
        edge_index = jax.random.randint(ks[1], (2, N_EDGES), 0, N_NODES, dtype=jnp.int64)
        edge_feature = jax.random.normal(ks[2], (N_EDGES, EDGE_DIM), dtype=jnp.float32)
        W_edge = jax.random.normal(ks[3], (EDGE_DIM, 1), dtype=jnp.float32) * (1.0 / np.sqrt(EDGE_DIM))
        b_edge = jnp.zeros((1,), dtype=jnp.float32)
        W_node = jax.random.normal(ks[4], (D_OUT, D_IN), dtype=jnp.float32) * (1.0 / np.sqrt(D_IN))
        b_node = jnp.zeros((D_OUT,), dtype=jnp.float32)
        return {'x': x, 'edge_index': edge_index, 'edge_feature': edge_feature, 'W_edge': W_edge, 'b_edge': b_edge, 'W_node': W_node, 'b_node': b_node}
    _L2_gnn_all = _L2_gnn_setup()
    _L2_gnn_in = {k: v for k, v in _L2_gnn_all.items() if k in ('W_edge', 'b_edge', 'W_node', 'b_node')}
    del _L2_gnn_all

    def _L3_gnn_setup():
        import jax, jax.numpy as jnp
        import numpy as np
        N_NODES = 3125
        N_EDGES = 1250000
        D_IN = 64
        D_HID = 64
        D_OUT = 64

        def sage_conv(x, edge_index, w_l, b_l, w_r):
            src, dst = (edge_index[0], edge_index[1])
            n = x.shape[0]
            msg_sum = jax.ops.segment_sum(x[src], dst, num_segments=n)
            deg = jax.ops.segment_sum(jnp.ones((src.shape[0],), x.dtype), dst, num_segments=n)
            mean = msg_sum / jnp.maximum(deg, 1.0)[:, None]
            return mean @ w_l + b_l + x @ w_r
        key = jax.random.key(seed)
        ks = jax.random.split(key, 8)
        x = jax.random.normal(ks[0], (N_NODES, D_IN), dtype=jnp.float32)
        edge_index = jax.random.randint(ks[1], (2, N_EDGES), 0, N_NODES, dtype=jnp.int64)
        s1 = 1.0 / np.sqrt(D_IN)
        s2 = 1.0 / np.sqrt(D_HID)
        w1_l = jax.random.uniform(ks[2], (D_IN, D_HID), jnp.float32, -s1, s1)
        w1_r = jax.random.uniform(ks[3], (D_IN, D_HID), jnp.float32, -s1, s1)
        b1 = jax.random.uniform(ks[4], (D_HID,), jnp.float32, -s1, s1)
        w2_l = jax.random.uniform(ks[5], (D_HID, D_OUT), jnp.float32, -s2, s2)
        w2_r = jax.random.uniform(ks[6], (D_HID, D_OUT), jnp.float32, -s2, s2)
        b2 = jax.random.uniform(ks[7], (D_OUT,), jnp.float32, -s2, s2)
        return {'x': x, 'edge_index': edge_index, 'w1_l': w1_l, 'b1': b1, 'w1_r': w1_r, 'w2_l': w2_l, 'b2': b2, 'w2_r': w2_r}
    _L3_gnn_all = _L3_gnn_setup()
    _L3_gnn_in = {k: v for k, v in _L3_gnn_all.items() if k in ('w1_l', 'b1', 'w1_r', 'w2_l', 'b2', 'w2_r')}
    del _L3_gnn_all
    return {'x': x, 'src': src, 'dst': dst, 'edge_attr_16': edge_attr_16, 'edge_weight1': edge_weight1, 'L0_gnn_W': _L0_gnn_in['W'], 'L0_gnn_b': _L0_gnn_in['b'], 'L0_gnn_gamma': _L0_gnn_in['gamma'], 'L0_gnn_beta': _L0_gnn_in['beta'], 'L1_gnn_W': _L1_gnn_in['W'], 'L1_gnn_b': _L1_gnn_in['b'], 'L1_gnn_W_lin': _L1_gnn_in['W_lin'], 'L1_gnn_b_lin': _L1_gnn_in['b_lin'], 'L2_gnn_W_edge': _L2_gnn_in['W_edge'], 'L2_gnn_b_edge': _L2_gnn_in['b_edge'], 'L2_gnn_W_node': _L2_gnn_in['W_node'], 'L2_gnn_b_node': _L2_gnn_in['b_node'], 'L3_gnn_w1_l': _L3_gnn_in['w1_l'], 'L3_gnn_b1': _L3_gnn_in['b1'], 'L3_gnn_w1_r': _L3_gnn_in['w1_r'], 'L3_gnn_w2_l': _L3_gnn_in['w2_l'], 'L3_gnn_b2': _L3_gnn_in['b2'], 'L3_gnn_w2_r': _L3_gnn_in['w2_r']}

def reference(x, src, dst, edge_attr_16, edge_weight1, L0_gnn_W, L0_gnn_b, L0_gnn_gamma, L0_gnn_beta, L1_gnn_W, L1_gnn_b, L1_gnn_W_lin, L1_gnn_b_lin, L2_gnn_W_edge, L2_gnn_b_edge, L2_gnn_W_node, L2_gnn_b_node, L3_gnn_w1_l, L3_gnn_b1, L3_gnn_w1_r, L3_gnn_w2_l, L3_gnn_b2, L3_gnn_w2_r):
    import jax
    import jax.numpy as jnp

    def _L0_gnn_ref(x, edge_index, edge_attr, W, b, gamma, beta):
        import jax, jax.numpy as jnp
        import numpy as np
        N_NODES = 3125
        N_EDGES = 50000
        D_IN = 64
        D_OUT = 64

        def _gcn_block(x, edge_index, edge_w, W, b, gamma, beta):
            n = x.shape[0]
            xw = x @ W
            loop = jnp.arange(n, dtype=edge_index.dtype)
            src = jnp.concatenate([edge_index[0], loop])
            dst = jnp.concatenate([edge_index[1], loop])
            w = jnp.concatenate([edge_w, jnp.ones((n,), dtype=x.dtype)])
            deg = jax.ops.segment_sum(w, dst, num_segments=n)
            dinv = jnp.where(deg > 0, jax.lax.rsqrt(deg), 0.0)
            norm = dinv[src] * w * dinv[dst]
            msg = xw[src] * norm[:, None]
            agg = jax.ops.segment_sum(msg, dst, num_segments=n)
            h = agg + b
            mu = jnp.mean(h, axis=-1, keepdims=True)
            var = jnp.mean(jnp.square(h - mu), axis=-1, keepdims=True)
            hn = (h - mu) * jax.lax.rsqrt(var + 1e-05) * gamma + beta
            return jax.nn.gelu(hn, approximate=False)
        edge_w = jnp.squeeze(edge_attr, axis=-1)
        return _gcn_block(x, edge_index, edge_w, W, b, gamma, beta)

    def _L1_gnn_ref(x, edge_index, W, b, W_lin, b_lin):
        import jax, jax.numpy as jnp
        import numpy as np
        N_NODES = 3125
        N_EDGES = 50000
        IN_DIM = 64
        OUT_DIM = 64

        def _gcn_conv(x, edge_index, W, b):
            n = x.shape[0]
            loop = jnp.arange(n, dtype=edge_index.dtype)
            src = jnp.concatenate([edge_index[0], loop])
            dst = jnp.concatenate([edge_index[1], loop])
            deg = jax.ops.segment_sum(jnp.ones_like(src, dtype=x.dtype), dst, num_segments=n)
            dinv = jax.lax.rsqrt(jnp.maximum(deg, 1.0))
            norm = dinv[src] * dinv[dst]
            h = x @ W
            msg = h[src] * norm[:, None]
            out = jax.ops.segment_sum(msg, dst, num_segments=n)
            return out + b
        return _gcn_conv(x, edge_index, W, b) + (x @ W_lin + b_lin)

    def _L2_gnn_ref(x, edge_index, edge_feature, W_edge, b_edge, W_node, b_node):
        import jax, jax.numpy as jnp
        import numpy as np
        N_NODES = 3125
        N_EDGES = 50000
        D_IN = 64
        D_OUT = 64
        EDGE_DIM = 16
        gate = jax.nn.sigmoid(edge_feature @ W_edge + b_edge)[:, 0]
        xp = x @ W_node.T + b_node
        row = edge_index[0]
        col = edge_index[1]
        num_nodes = x.shape[0]
        msg = gate[:, None] * xp[col]
        summed = jax.ops.segment_sum(msg, row, num_segments=num_nodes)
        cnt = jax.ops.segment_sum(jnp.ones((row.shape[0],), dtype=xp.dtype), row, num_segments=num_nodes)
        out = summed / jnp.maximum(cnt, 1.0)[:, None]
        return out

    def _L3_gnn_ref(x, edge_index, w1_l, b1, w1_r, w2_l, b2, w2_r):
        import jax, jax.numpy as jnp
        import numpy as np
        N_NODES = 3125
        N_EDGES = 1250000
        D_IN = 64
        D_HID = 64
        D_OUT = 64

        def sage_conv(x, edge_index, w_l, b_l, w_r):
            src, dst = (edge_index[0], edge_index[1])
            n = x.shape[0]
            msg_sum = jax.ops.segment_sum(x[src], dst, num_segments=n)
            deg = jax.ops.segment_sum(jnp.ones((src.shape[0],), x.dtype), dst, num_segments=n)
            mean = msg_sum / jnp.maximum(deg, 1.0)[:, None]
            return mean @ w_l + b_l + x @ w_r
        h = jax.nn.relu(sage_conv(x, edge_index, w1_l, b1, w1_r))
        return sage_conv(h, edge_index, w2_l, b2, w2_r)
    edge_index = jnp.stack([src, dst])
    h = jnp.maximum(_layernorm(x, axis=-1), 0.0)
    x = x + _L0_gnn_ref(h, edge_index, edge_weight1, L0_gnn_W, L0_gnn_b, L0_gnn_gamma, L0_gnn_beta)
    h = jnp.maximum(_layernorm(x, axis=-1), 0.0)
    x = x + _L1_gnn_ref(h, edge_index, L1_gnn_W, L1_gnn_b, L1_gnn_W_lin, L1_gnn_b_lin)
    h = jnp.maximum(_layernorm(x, axis=-1), 0.0)
    x = x + _L2_gnn_ref(h, edge_index, edge_attr_16, L2_gnn_W_edge, L2_gnn_b_edge, L2_gnn_W_node, L2_gnn_b_node)
    h = jnp.maximum(_layernorm(x, axis=-1), 0.0)
    x = x + _L3_gnn_ref(h, edge_index, L3_gnn_w1_l, L3_gnn_b1, L3_gnn_w1_r, L3_gnn_w2_l, L3_gnn_b2, L3_gnn_w2_r)
    return x

_drawn_inputs = setup_inputs


def setup_inputs(seed=0):
    import zlib

    import numpy as np

    out = dict(_drawn_inputs(seed))
    spreads = {'L0_gnn_b': (0.0, 0.1),
     'L0_gnn_gamma': (1.0, 0.2),
     'L0_gnn_beta': (0.0, 0.1),
     'L2_gnn_b_node': (0.0, 0.1)}
    factors = {}
    for name, (base, spread) in spreads.items():
        noise = np.random.default_rng([zlib.crc32(name.encode()), seed]).standard_normal(out[name].shape)
        drawn = base * np.exp(spread * noise) if base else spread * noise
        out[name] = jnp.asarray(drawn.astype(out[name].dtype))
    for name, factor in factors.items():
        out[name] = (out[name] * factor).astype(out[name].dtype)
    return out
```

```python
import concourse.bass as bass
from concourse import mybir
from contextlib import ExitStack

N = 3125
F = 64
E = 103125
EDGE_F = 16
P = 128
T = -(-N // P)
TAIL = N - (T - 1) * P
C = -(-E // P)
E_TAIL = E - (P - 1) * C
B = T * T
HALF = P
ROWS2 = 2 * HALF * B
ROWS = ROWS2 + HALF * T
CH = 2 * B + T
G = 13
GROUPS = C // G
assert GROUPS * G == C and GROUPS % 2 == 0
K = 2 * T + 1
QUADS = -(-K // 4)
KP = 4 * QUADS
MSG_QUADS = [2, 2, 2, 2, 2, 1, 1, 1]
assert sum(MSG_QUADS) == QUADS
NG = len(MSG_QUADS)
FIRST = [4 * sum(MSG_QUADS[:g]) for g in range(NG + 1)]
TC = T + 1
AHEAD = NG + 1
RING = 5
assert T % RING == 0 and T % 2 == 1
FAR = 1.0e6
EPS = 1e-5

f32, bf16, f16, i32 = mybir.dt.float32, mybir.dt.bfloat16, mybir.dt.float16, mybir.dt.int32
ALU = mybir.AluOpType
ACT = mybir.ActivationFunctionType
AX = mybir.AxisListType



def gnn(nc, x, src, dst, edge_attr, edge_w, w0, b0, gamma, beta, w1, b1, wlin, blin,
        wedge, bedge, wnode, bnode, w3l, b3, w3r, w4l, b4, w4r, out, slots, count_table, rows_table, added_table,
        marks_table, fields_table):
    ctx = ExitStack()
    with ctx:
        def sb(name, shape, dt=f32):
            return ctx.enter_context(nc.sbuf_tensor(name, shape, dt))

        def sem(name):
            return ctx.enter_context(nc.semaphore(name))

        src_i = sb("src_i", [P, C], i32)
        dst_i = sb("dst_i", [P, C], i32)
        payload = sb("payload", [P, C, 4])
        work = sb("work", [P, 6 * C + 1])
        w_in, src_t, dst_t, third, rank = [work[:, n * C:(n + 1) * C] for n in range(5)]
        key = work[:, 5 * C:6 * C + 1]
        sum_f = work[:, 0:2 * 1024].rearrange("p (r e) -> p r e", r=2)
        gat_t = work[:, 2048:2048 + 1024].bitcast(bf16).rearrange("p (r e) -> p r e", r=2)
        msg = work[:, 3072:3072 + 1024].rearrange("p (r c f) -> p r c f", r=2, c=8)
        tht = work[:, 0:2 * 4 * P].rearrange("p (r e) -> p r e", r=2)
        iota_b = sb("iota_b", [P, B], f16)
        sorting = sb("sorting", [P, G * B + 1], bf16)
        onehot = sorting[:, 0:G * B].rearrange("p (a b) -> p a b", a=G)
        TH = sorting[:, 0:2 * T * 2 * F].bitcast(f32).rearrange("p (t f) -> p t f", t=T)
        scratch = sb("scratch", [P, 2 * B], bf16)
        junk = scratch[:, :].rearrange("p (r b) -> p r b", r=2)
        added_rows = TH[:, :, 0:F]
        added_sums = scratch[:, 0:4 * T].bitcast(f32).rearrange("p (t f) -> p t f", f=2)
        edge_row = sb("edge_row", [1, F + 2])
        edge_dst = sb("edge_dst", [1, 1], i32)
        left_over = sb("left_over", [P, 1])
        left_b = sb("left_b", [P, 1], bf16)
        left_i = sb("left_i", [P, 1], i32)
        before = sb("before", [P, P], bf16)
        after = sb("after", [P, P], bf16)
        ones = sb("ones", [P, P], bf16)
        pos = sb("pos", [P, 4, G])
        place = sb("place", [P, 2, G], i32)
        pay = sb("pay", [P, 2, G, 4])
        slot = sb("slot", [P, CH, 4])
        cnt_out = slot[:, :, :].rearrange("p c f -> p (c f)")[:, 0:TC * P].bitcast(bf16).rearrange(
            "p (r n) -> p r n", r=2)
        near = [sb("near_src", [P, T, KP], bf16), sb("near_dst", [P, T, KP], bf16)]
        far = [sb("far_src", [P, T, KP], bf16), sb("far_dst", [P, T, KP], bf16)]
        wgt = [sb("wgt_src", [P, T, KP]), sb("wgt_dst", [P, T, KP])]
        wparts = sb("wparts", [P, T, KP, 4], bf16)
        iota_f = sb("iota_f", [P, P], f16)
        iota_4 = sb("iota_4", [P, P, 4], bf16)
        iota_p = sb("iota_p", [P, 1])
        ident_h = sb("ident_h", [P, P], bf16)
        ident_f = sb("ident_f", [P, P])
        OH = QUADS * P * 4
        big = sb("big", [P, 2 * OH])
        attr = big[:, 0:C * EDGE_F].rearrange("p (c f) -> p c f", f=EDGE_F)
        oh = big[:, :].bitcast(bf16).rearrange("p (r s q l c) -> p r s q l c", r=2, s=2, q=QUADS, c=4)
        cnt_in = big[:, 0:RING * TC * P // 2].bitcast(bf16).rearrange("p (r n) -> p r n", r=RING)
        X = sb("X", [P, T, F])
        H = TH[:, :, F:2 * F]
        V = sb("V", [P, T, F])
        U = sb("U", [P, T, F])
        marks = U[:, :, :].rearrange("p t f -> p (t f)")[0:1, 0:C].bitcast(i32)
        agg = sb("agg", [P, T, F + 4])
        sq = agg[:, :, 0:F]
        tmp_i = agg[:, :, :].rearrange("p t f -> p (t f)")[:, 0:C].bitcast(i32)
        parts = sb("parts", [P, T, 3, F], bf16)
        stat = sb("stat", [P, 4, T])
        deg = sb("deg", [P, T, 4])
        wsum = sb("wsum", [P, T])
        gsum = sb("gsum", [P, T])
        dinv = sb("dinv", [P, 2, T])
        icnt = sb("icnt", [P, 2, T])
        wedge_b = sb("wedge_b", [P, EDGE_F])
        bedge_b = sb("bedge_b", [P, 1])
        WS = sb("WS", [P, 5, F])
        bias = sb("bias", [P, 7, F])
        wn = sb("wn", [F, F])

        counts = [ctx.enter_context(nc.psum_tensor(f"counts{a}", [P, 2, 512], f32)) for a in range(2)]
        turned_oh = [ctx.enter_context(nc.psum_tensor(f"turned_oh{a}", [P, 1024], bf16)) for a in range(2)]
        acc = [ctx.enter_context(nc.psum_tensor(f"acc{a}", [P, 512], f32)) for a in range(2)]
        tiles = gat = turn = [counts[0][:, 0, :], counts[0][:, 1, :]]
        proj = [counts[1][:, 0, :], counts[1][:, 1, :]]

        cleared = sem("cleared")
        nodes_cleared = sem("nodes_cleared")
        edges_in = sem("edges_in")
        attrs_in = sem("attrs_in")
        small_in = sem("small_in")
        nodes_in = sem("nodes_in")
        weights_in = sem("weights_in")
        iotas = sem("iotas")
        consts = sem("consts")
        dve_step = sem("dve_step")
        gate_sum = sem("gate_sum")
        gates = sem("gates")
        payloads = sem("payloads")
        oh_ready = sem("oh_ready")
        rank_ready = sem("rank_ready")
        rank_read = sem("rank_read")
        placed = sem("placed")
        place_step = sem("place_step")
        wparts_ready = sem("wparts_ready")
        oh_made = sem("oh_made")
        paid = sem("paid")
        scattered = [sem("scattered0"), sem("scattered1")]
        sorted_in = sem("sorted_in")
        left_counted = sem("left_counted")
        left_summed = sem("left_summed")
        left_known = sem("left_known")
        corrected = sem("corrected")
        fix_step = sem("fix_step")
        fix_moved = sem("fix_moved")
        edge_in = sem("edge_in")
        marks_in = sem("marks_in")
        dst_in = sem("dst_in")
        edge_scaled = sem("edge_scaled")
        edge_added = sem("edge_added")
        tiles_full = sem("tiles_full")
        tiles_read = sem("tiles_read")
        block_out = sem("block_out")
        block_sent = sem("block_sent")
        counted = sem("counted")
        counts_read = sem("counts_read")
        counts_in = [sem(f"counts_in{r}") for r in range(RING)]
        deg_read = sem("deg_read")
        parts_ready = sem("parts_ready")
        oh_turned = sem("oh_turned")
        gat_ready = sem("gat_ready")
        sum_ready = sem("sum_ready")
        gathered = sem("gathered")
        msg_ready = sem("msg_ready")
        summed = sem("summed")
        agg_ready = sem("agg_ready")
        th_ready = sem("th_ready")
        turned = sem("turned")
        tht_ready = sem("tht_ready")
        projected = sem("projected")
        proj_read = sem("proj_read")
        sqrt_in = sem("sqrt_in")
        sqrt_out = sem("sqrt_out")
        gelu_in = sem("gelu_in")
        gelu_out = sem("gelu_out")
        wn_turned = sem("wn_turned")
        wn_ready = sem("wn_ready")
        result = sem("result")
        stored = sem("stored")

        PRESET = 1
        SRC, DST = 0, 1
        WEIGHTED = {0: DST, 2: SRC}
        COUNTED = (1, 3, 4)
        NQ = -(-T // 4)

        def slot_parts():
            yield (slot[:, 0:2 * B, :].rearrange("p (q b) f -> p q (b f)", q=2),
                   slots[0:ROWS2, :].rearrange("(q p b) f -> p q (b f)", q=2, p=P))
            yield (slot[:, 2 * B:CH, :].rearrange("p b f -> p (b f)"),
                   slots[ROWS2:ROWS, :].rearrange("(p b) f -> p (b f)", p=P))

        def in_pairs(eng, body):
            with eng.Fori(0, T // 2) as it:
                body([(2 * it, 0), (2 * it + 1, 1)])
            body([(T - 1, 0)])

        def tile(ap, o):
            return ap[:, bass.ds(o, 1)]

        block = ctx.enter_context(nc.Block())

        @block.sync
        def _(sp):
            m = (P - 1) * C
            sp.wait_ge(cleared, 1)
            for ap, to in ((src, src_i), (dst, dst_i)):
                sp.dma_start(to[0:P - 1, :], ap[0:m].rearrange("(p c) -> p c", p=P - 1)).then_inc(edges_in, 16)
                sp.dma_start(to[P - 1:P, 0:E_TAIL], ap[m:E].rearrange("(a c) -> a c", a=1)).then_inc(edges_in, 16)
            sp.dma_start(attr[0:P - 1, :, :], edge_attr[0:m, :].rearrange("(p c) f -> p c f", p=P - 1)).then_inc(attrs_in, 16)
            sp.dma_start(attr[P - 1:P, 0:E_TAIL, :], edge_attr[m:E, :].rearrange("(p c) f -> p c f", p=1)).then_inc(attrs_in, 16)
            sp.dma_start(w_in[0:P - 1, :], edge_w[0:m, :].rearrange("(p c) a -> p (c a)", p=P - 1)).then_inc(edges_in, 16)
            sp.dma_start(w_in[P - 1:P, 0:E_TAIL], edge_w[m:E, :].rearrange("(p c) a -> p (c a)", p=1)).then_inc(edges_in, 16)
            sp.wait_ge(nodes_cleared, 1)
            sp.dma_start(X[:, 0:T - 1, :], x[0:(T - 1) * P, :].rearrange("(t p) f -> p t f", p=P)).then_inc(nodes_in, 16)
            sp.dma_start(X[0:TAIL, T - 1, :], x[(T - 1) * P:N, :]).then_inc(nodes_in, 16)
            for l, (top, bottom) in enumerate(((w0, None), (w1, wlin), (None, None), (w3l, w3r), (w4l, w4r))):
                if top is not None:
                    sp.dma_start(WS[0:F, l, :], top).then_inc(weights_in, 16)
                if bottom is not None:
                    sp.dma_start(WS[F:2 * F, l, :], bottom).then_inc(weights_in, 16)
            sp.dma_start(wn[:, :], wnode).then_inc(weights_in, 16)
            sp.dma_start(WS[F:F + 1, 2, :], bnode.rearrange("(a n) -> a n", a=1)).then_inc(weights_in, 16)
            for n, ap in enumerate((b0, b1, b3, b4, gamma, beta, blin)):
                sp.dma_start(bias[:, n, :], ap.rearrange("(a n) -> a n", a=1).to_broadcast([P, F])).then_inc(weights_in, 16)
            for s in range(2):
                sp.wait_ge(scattered[s], 16 + 16 * G * (GROUPS // 2))
            for here, there in slot_parts():
                sp.dma_start(here, there).then_inc(sorted_in, 16)

            def send(os):
                for o, j in os:
                    sp.wait_ge(tiles_read, AHEAD + NG * (o + 1))
                    sp.dma_start(count_table[bass.ds(o, 1), :, :].rearrange("a p n -> p (a n)"),
                                 cnt_out[:, j, :]).then_inc(block_out, 16)
                    sp.wait_ge(block_out, 16 * (o + 1))
                    sp.sem_inc(block_sent, 1)

            in_pairs(sp, send)
            for n, l in enumerate(COUNTED):
                sp.wait_ge(parts_ready, l + 1)
                with sp.Fori(0, T // RING) as it:
                    for r in range(RING):
                        sp.wait_ge(counted, AHEAD + n * T + RING * it + r - RING + 1)
                        sp.dma_start(cnt_in[:, r, :],
                                     count_table[bass.ds(it * RING + r, 1), :, :].rearrange("a p n -> p (a n)"))\
                          .then_inc(counts_in[r], 16)
            sp.wait_ge(result, 1)
            sp.dma_start(out[0:(T - 1) * P, :].rearrange("(t p) f -> p t f", p=P), X[:, 0:T - 1, :]).then_inc(stored, 16)
            sp.dma_start(out[(T - 1) * P:N, :], X[0:TAIL, T - 1, :]).then_inc(stored, 16)
            sp.wait_ge(stored, 32)

        WEIGHTS = 16 * (7 + 2 + 7)

        @block.gpsimd
        def _(pool):
            pool.iota(tmp_i[:, :], [[1, C]], base=0, channel_multiplier=C).then_inc(iotas, 1)
            pool.iota(iota_f[:, :], [[1, P]], base=0, channel_multiplier=0,
                      allow_small_or_imprecise_dtypes=True).then_inc(iotas, 1)
            pool.iota(iota_p[:, :], [[0, 1]], base=0, channel_multiplier=1,
                      allow_small_or_imprecise_dtypes=True).then_inc(iotas, 1)
            pool.iota(iota_b[:, :], [[1, B]], base=0, channel_multiplier=0,
                      allow_small_or_imprecise_dtypes=True).then_inc(iotas, 1)
            pool.iota(iota_4[:, :, :], [[1, P], [0, 4]], base=0, channel_multiplier=0,
                      allow_small_or_imprecise_dtypes=True).then_inc(iotas, 1)
            pool.memset(slot[:, :, 0:2], -1.0).then_inc(iotas, 1)
            pool.memset(slot[:, :, 2:4], 0.0).then_inc(iotas, 1)
            pool.wait_ge(iotas, 7)
            for s, (here, there) in enumerate(slot_parts()):
                pool.dma_start(there, here).then_inc(scattered[s], 16)
            for side in range(2):
                pool.memset(near[side][:, :, :], -1.0)
                pool.memset(far[side][:, :, :], -1.0)
            pool.memset(WS[:, :, :], 0.0)
            pool.memset(X[:, :, :], 0.0).then_inc(nodes_cleared, 1)
            pool.wait_ge(scattered[0], 16)
            pool.wait_ge(scattered[1], 16)
            last_row = pool.to_reg(ROWS - 1)
            group = pool.alloc_register("group")
            pool.reg_mov(group, 1)
            with pool.Fori(0, GROUPS // 2) as it:
                for s in range(2):
                    pool.reg_add(group, group, 1)
                    pool.wait_ge(iotas, 7)
                    pool.wait_ge(placed, group)
                    pool.wait_ge(paid, group)
                    for u in range(G):
                        pool.indirect_dma_start(slots, bass.IndirectOffsetOnAxis(ap=place[:, s, u:u + 1], axis=0),
                                                pay[:, s, u, :], None, bounds_check=last_row,
                                                oob_is_err=False).then_inc(scattered[s], 16)

            pool.wait_ge(left_known, 1)
            left = pool.value_load(left_i[0:1, 0:1])
            steps, moves = [0], [0]

            def link(ins):
                steps[0] += 1
                ins.then_inc(fix_step, 1)
                pool.wait_ge(fix_step, steps[0])

            def move(to, here, **how):
                moves[0] += 1
                pool.dma_start(to, here, **how).then_inc(fix_moved, 16)
                pool.wait_ge(fix_moved, 16 * moves[0])

            def by_tile(table):
                return table[1:T * P + 1, :].rearrange("(t p) f -> p t f", p=P)

            def add_edges(side, weight, rows):
                link(pool.memset(edge_row[:, :], 1.0))
                link(pool.memset(added_rows, 0.0))
                link(pool.memset(added_sums, 0.0))
                move(by_tile(added_table[:, 0:F]), added_rows)
                move(by_tile(added_table[:, F:F + 2]), added_sums)
                if rows is not None:
                    move(by_tile(rows_table), rows)
                with pool.Fori(0, P) as p:
                    pool.dma_start(marks, marks_table[0, bass.ds(p, 1), :]).then_inc(marks_in, 16)
                    pool.wait_ge(marks_in, 16)
                    pool.sem_clear(marks_in)
                    with pool.Fori(0, C) as c:
                        marked = pool.value_load(marks[0:1, bass.ds(c, 1)], min_val=0, max_val=N)
                        with pool.If(marked > 0):
                            pool.dma_start(edge_dst[:, :], marks_table[1, bass.ds(p, 1), bass.ds(c, 1)]).then_inc(dst_in, 16)
                            pool.wait_ge(dst_in, 16)
                            ends = pool.value_load(edge_dst[0:1, 0:1], min_val=1, max_val=N)
                            there, here = (marked, ends) if side == DST else (ends, marked)
                            pool.dma_start(edge_row[0:1, F + 1:F + 2],
                                           fields_table[bass.ds(p * C + c, 1), weight:weight + 1]).then_inc(edge_in, 16)
                            if rows is not None:
                                pool.dma_start(edge_row[0:1, 0:F], rows_table[bass.ds(there, 1), :]).then_inc(edge_in, 16)
                            pool.wait_ge(edge_in, 16 if rows is None else 32)
                            if l in WEIGHTED:
                                pool.tensor_tensor(edge_row[0:1, 0:F], edge_row[0:1, 0:F],
                                                   edge_row[0:1, F + 1:F + 2].to_broadcast([1, F]), ALU.mult)\
                                    .then_inc(edge_scaled, 1)
                                pool.wait_ge(edge_scaled, 1)
                            pool.dma_start(added_table[bass.ds(here, 1), :], edge_row[0:1, :],
                                           accum_op=ALU.add).then_inc(edge_added, 16)
                            pool.wait_ge(edge_added, 16)
                            for used in (dst_in, edge_in, edge_scaled, edge_added):
                                pool.sem_clear(used)
                move(added_rows, by_tile(added_table[:, 0:F]))
                move(added_sums, by_tile(added_table[:, F:F + 2]))

            l = None
            pool.wait_ge(deg_read, AHEAD + T)
            with pool.If(left > 0):
                move(marks_table[0, :, :], src_i[:, :])
                move(marks_table[1, :, :], dst_i[:, :])
                move(fields_table.rearrange("(p c) f -> p c f", p=P), payload[:, :, :])
                add_edges(DST, 2, None)
                link(pool.tensor_tensor(deg[:, :, 0:2], deg[:, :, 0:2], added_sums, ALU.add))
            pool.sem_inc(corrected, 1)
            weighted = counted_layers = 0
            for l in range(5):
                pool.wait_ge(parts_ready, l + 1)
                if l in WEIGHTED:
                    weighted += 1
                    pool.wait_ge(agg_ready, AHEAD + weighted * T)
                else:
                    counted_layers += 1
                    pool.wait_ge(counts_read, AHEAD + counted_layers * T)
                with pool.If(left > 0):
                    add_edges(WEIGHTED.get(l, DST), 3 if l == 2 else 2, V[:, :, :] if l < 2 else H)
                    link(pool.tensor_tensor(agg[:, :, 0:F], agg[:, :, 0:F], added_rows, ALU.add))
                    if l == 2:
                        link(pool.tensor_tensor(agg[:, :, F:F + 2], agg[:, :, F:F + 2], added_sums, ALU.add))
                pool.sem_inc(corrected, 1)

        @block.scalar
        def _(act):
            act.dma_start(wedge_b[:, :], wedge.rearrange("k a -> a k").to_broadcast([P, EDGE_F])).then_inc(small_in, 16)
            act.dma_start(bedge_b[:, :], bedge.rearrange("(a n) -> a n", a=1).to_broadcast([P, 1])).then_inc(small_in, 16)
            act.wait_ge(gate_sum, 1)
            act.wait_ge(small_in, 32)
            act.activation(payload[:, :, 3], third, ACT.Sigmoid, bias=bedge_b[:, 0:1]).then_inc(gates, 1)
            act.wait_ge(gates, 1)
            act.wait_ge(payloads, 1)
            act.sem_inc(paid, PRESET)
            with act.Fori(0, GROUPS // 2) as it:
                for s in range(2):
                    act.wait_ge(scattered[s], 16 + 16 * G * it)
                    act.copy(pay[:, s, :, :], payload[:, bass.ds((2 * it + s) * G, G), :]).then_inc(paid, 1)

            def root(n):
                act.wait_ge(sqrt_in, n + 1)
                act.activation(stat[:, 2, :], stat[:, 1, :], ACT.Sqrt).then_inc(sqrt_out, 1)

            act.wait_ge(wn_turned, 1)
            act.copy(WS[0:F, 2, :], acc[1][0:F, 0:F]).then_inc(wn_ready, 1)

            def blocks(os):
                for o, j in os:
                    for g in range(NG):
                        n = o * NG + g
                        lo, w = FIRST[g] // 2 * P, 2 * MSG_QUADS[g] * P
                        act.wait_ge(tiles_full, AHEAD + n + 1)
                        if g == 0:
                            act.wait_ge(block_sent, AHEAD + o - 1)
                        act.copy(cnt_out[:, j, lo:lo + w], tiles[g % 2][:, 0:w]).then_inc(tiles_read, 1)
                    act.copy(tile(deg, o), acc[j][:, 0:4]).then_inc(deg_read, 1)

            act.sem_inc(block_sent, AHEAD)
            in_pairs(act, blocks)
            for n in range(3):
                root(n)
            weighted = 0
            for l in range(5):
                if l in WEIGHTED:
                    width = F if l == 0 else F + 4

                    def group(l, m, o, j, g):
                        n = m * NG + g
                        w = min(K, FIRST[g + 1]) - FIRST[g]
                        q = MSG_QUADS[g]
                        act.wait_ge(oh_turned, n + 1)
                        act.wait_ge(gathered, AHEAD + n - 1)
                        act.copy(gat_t[:, g % 2, 0:w * P], turned_oh[g % 2][:, 0:w * P]).then_inc(gat_ready, 1)
                        act.wait_ge(oh_made, (T + m) * NG + g + 1)
                        act.wait_ge(summed, AHEAD + n - 1)
                        act.copy(sum_f[:, g % 2, 0:4 * q * P].rearrange("p (q c l) -> p q c l", q=q, c=4),
                                 oh[:, j, 1, FIRST[g] // 4:FIRST[g] // 4 + q, :, :].rearrange("p q l c -> p q c l"))\
                           .then_inc(sum_ready, 1)

                    def take(m, o, j):
                        act.wait_ge(summed, AHEAD + (m + 1) * NG)
                        act.copy(tile(agg, o)[:, :, 0:width].rearrange("p a f -> p (a f)"),
                                 acc[j][:, 0:width]).then_inc(agg_ready, 1)

                    def groups(os):
                        for i, (o, j) in enumerate(os):
                            m = weighted * T + o
                            for g in range(NG):
                                group(l, m, o, j, g)
                                if g == 0 and i:
                                    take(m - 1, *os[0])
                            if i == len(os) - 1:
                                take(m, o, j)

                    in_pairs(act, groups)
                    weighted += 1
                for q in range(NQ):
                    n = NQ * l + q
                    w = min(4, T - 4 * q) * P
                    act.wait_ge(turned, n + 1)
                    if n >= 2:
                        act.wait_ge(projected, n - 1)
                    act.copy(tht[:, n % 2, 0:w], turn[n % 2][:, 0:w]).then_inc(tht_ready, 1)
                if l == 0:
                    root(3)
                    act.wait_ge(gelu_in, 1)
                    act.activation(U[:, :, :], V[:, :, :], ACT.Gelu).then_inc(gelu_out, 1)
                if l < 3:
                    root(4 + l)

        @block.vector
        def _(dve):
            step = [0]
            roots = [0]

            def link(ins):
                step[0] += 1
                ins.then_inc(dve_step, 1)
                dve.wait_ge(dve_step, step[0])

            def rows(ap, width=F):
                return ap.unsqueeze(2).to_broadcast([P, ap.shape[1], width])

            def root():
                roots[0] += 1
                dve.wait_ge(sqrt_out, roots[0])
                link(dve.reciprocal(stat[:, 3, :], stat[:, 2, :]))

            def normed(a):
                link(dve.tensor_reduce(stat[:, 0, :], a, AX.X, ALU.add))
                link(dve.tensor_scalar(stat[:, 0, :], stat[:, 0, :], -1.0 / F, None, ALU.mult))
                link(dve.tensor_tensor(V[:, :, :], a, rows(stat[:, 0, :]), ALU.add))
                link(dve.tensor_tensor(sq, V[:, :, :], V[:, :, :], ALU.mult))
                link(dve.tensor_reduce(stat[:, 1, :], sq, AX.X, ALU.add))
                dve.tensor_scalar(stat[:, 1, :], stat[:, 1, :], 1.0 / F, EPS, ALU.mult, ALU.add).then_inc(sqrt_in, 1)
                root()

            def split(a, out, rest):
                link(dve.tensor_copy(out(0), a))
                link(dve.tensor_tensor(rest, a, out(0), ALU.subtract))
                link(dve.tensor_copy(out(1), rest))
                link(dve.tensor_tensor(rest, rest, out(1), ALU.subtract))
                return dve.tensor_copy(out(2), rest)

            dve.memset(src_i[:, E_TAIL:C], 0)
            dve.memset(dst_i[:, E_TAIL:C], 0)
            dve.memset(attr[:, E_TAIL:C, :], 0.0)
            dve.memset(w_in[:, E_TAIL:C], 0.0).then_inc(cleared, 1)
            dve.memset(onehot[:, G - 2:G, :], 0.0)
            dve.memset(ones[:, :], 1.0)
            dve.wait_ge(iotas, 3)
            dve.tensor_scalar(ident_h[:, :], iota_f[:, :], iota_p[:, 0:1], None, ALU.is_equal)
            dve.tensor_scalar(ident_f[:, :], iota_f[:, :], iota_p[:, 0:1], None, ALU.is_equal)
            dve.tensor_scalar(before[:, :], iota_f[:, :], iota_p[:, 0:1], None, ALU.is_gt)
            dve.tensor_scalar(after[:, :], iota_f[:, :], iota_p[:, 0:1], None, ALU.is_le).then_inc(consts, 1)
            link(dve.tensor_scalar(rank, tmp_i[:, :], float(E), FAR, ALU.is_ge, ALU.mult))
            dve.wait_ge(edges_in, 96)
            for ids_i, to, field in ((src_i, src_t, 0), (dst_i, dst_t, 1)):
                link(dve.tensor_scalar(tmp_i[:, :], ids_i[:, :], 7, None, ALU.logical_shift_right))
                link(dve.tensor_copy(to, tmp_i[:, :]))
                link(dve.tensor_scalar(tmp_i[:, :], ids_i[:, :], P - 1, None, ALU.bitwise_and))
                link(dve.tensor_copy(payload[:, :, field], tmp_i[:, :]))
            dve.memset(key[:, C:C + 1], FAR)
            dve.tensor_copy(payload[:, :, 2], w_in)
            link(dve.scalar_tensor_tensor(out=key[:, 0:C], in0=src_t, scalar=float(T), in1=dst_t,
                                          op0=ALU.mult, op1=ALU.add))
            link(dve.tensor_tensor(key[:, 0:C], key[:, 0:C], rank, ALU.add))
            dve.wait_ge(small_in, 32)
            dve.wait_ge(attrs_in, 32)
            link(dve.tensor_tensor(attr, attr, wedge_b[:, :].unsqueeze(1).to_broadcast([P, C, EDGE_F]), ALU.mult))
            dve.tensor_reduce(third, attr, AX.X, ALU.add).then_inc(gate_sum, 1)
            dve.wait_ge(gates, 1)
            link(dve.tensor_tensor(w_in, src_t, dst_t, ALU.not_equal))
            link(dve.scalar_tensor_tensor(out=third, in0=w_in, scalar=FAR, in1=src_t, op0=ALU.mult, op1=ALU.add))
            dve.tensor_scalar(third, third, float(ROWS2 - 2 * P * T), None, ALU.add).then_inc(payloads, 1)
            dve.wait_ge(payloads, 1)

            def place_steps(it, s):
                cols = bass.ds((2 * it + s) * G, G)
                at = PRESET + (2 * it + s) * 4

                def step0():
                    dve.wait_ge(rank_read, 2 + 2 * G * it + G * (s + 1))
                    dve.wait_ge(placed, PRESET + 2 * it + s)
                    dve.tensor_scalar(pos[:, 0, :], rank[:, cols], 3.0 * P, None, ALU.min).then_inc(place_step, 1)

                def step1():
                    dve.wait_ge(place_step, at + 1)
                    dve.scalar_tensor_tensor(out=pos[:, 1, :], in0=pos[:, 0, :], scalar=float(B), in1=key[:, cols],
                                             op0=ALU.mult, op1=ALU.add)
                    dve.scalar_tensor_tensor(out=pos[:, 2, :], in0=pos[:, 0, :], scalar=float(T), in1=third[:, cols],
                                             op0=ALU.mult, op1=ALU.add).then_inc(place_step, 1)

                def step2():
                    dve.wait_ge(place_step, at + 2)
                    dve.tensor_tensor(pos[:, 3, :], pos[:, 2, :], pos[:, 1, :], ALU.subtract).then_inc(place_step, 1)

                def step3():
                    dve.wait_ge(place_step, at + 3)
                    dve.scalar_tensor_tensor(out=pos[:, 2, :], in0=pos[:, 0, :], scalar=2.0 * P, in1=pos[:, 3, :],
                                             op0=ALU.is_ge, op1=ALU.mult).then_inc(place_step, 1)

                def step4():
                    dve.wait_ge(place_step, at + 4)
                    dve.wait_ge(scattered[s], 16 + 16 * G * it)
                    dve.tensor_tensor(place[:, s, :], pos[:, 1, :], pos[:, 2, :], ALU.add).then_inc(placed, 1)

                return [step0, step1, step2, step3, step4]

            dve.sem_inc(place_step, PRESET)
            dve.sem_inc(placed, PRESET)
            dve.memset(junk[:, 0, :], 0.0).then_inc(rank_read, 2)

            def mark(col, v):
                dve.tensor_scalar(onehot[:, v % G, :], iota_b[:, :], key[:, bass.ds(col, 1)], None,
                                  ALU.is_equal).then_inc(oh_ready, 1)

            dve.wait_ge(iotas, 4)
            mark(0, 0)
            with dve.Fori(0, GROUPS // 2) as it:
                steps = []
                for v in range(2 * G):
                    mark(2 * G * it + v + 1, v + 1)
                    dve.wait_ge(rank_ready, 2 * G * it + v + 1)
                    dve.scalar_tensor_tensor(out=junk[:, v % 2, :],
                                             in0=counts[v % 2][:, :, :].rearrange("p a b -> p (a b)")[:, 0:B],
                                             scalar=1.0, in1=onehot[:, v % G, :], op0=ALU.mult, op1=ALU.mult,
                                             accum_out=rank[:, bass.ds(2 * G * it + v, 1)]).then_inc(rank_read, 1)
                    if v == G:
                        steps = place_steps(it, 0)
                    elif steps:
                        steps.pop(0)()
                steps = place_steps(it, 1)
                for s in steps:
                    s()

            dve.wait_ge(rank_read, 2 + C)
            link(dve.scalar_tensor_tensor(out=third, in0=w_in, scalar=float(P), in1=rank, op0=ALU.mult, op1=ALU.add))
            dve.tensor_scalar(third, third, 3.0 * P, None, ALU.is_ge)
            dve.tensor_scalar(dst_i[:, :], dst_i[:, :], 1, None, ALU.add)
            link(dve.tensor_scalar(src_i[:, :], src_i[:, :], 1, None, ALU.add))
            dve.tensor_tensor(src_i[:, :], src_i[:, :], third, ALU.mult)
            link(dve.tensor_reduce(left_over[:, :], third, AX.X, ALU.add))
            dve.tensor_copy(left_b[:, :], left_over[:, :]).then_inc(left_counted, 1)
            dve.wait_ge(left_summed, 1)
            dve.tensor_copy(left_i[:, :], acc[0][:, 0:1]).then_inc(left_known, 1)

            dve.wait_ge(sorted_in, 32)
            for q in range(3):
                if q < 2:
                    plane = slot[:, q * B:(q + 1) * B, :]
                    view = [lambda f, plane=plane: plane[:, :, f].rearrange("p (o t) -> p o t", o=T),
                            lambda f, plane=plane: plane[:, :, f].rearrange("p (t o) -> p o t", o=T)]
                    cols = slice(q, 2 * T, 2)
                else:
                    view = [lambda f: slot[:, 2 * B:CH, f].unsqueeze(2)] * 2
                    cols = slice(2 * T, K)
                for side in (DST, SRC):
                    dve.tensor_copy(near[side][:, :, cols], view[side](side))
                    dve.tensor_copy(far[side][:, :, cols], view[side](1 - side))
                    ins = dve.tensor_copy(wgt[side][:, :, cols], view[side](2 if side == DST else 3))
            link(ins)
            dve.memset(wparts[:, :, :, 0], 1.0)
            rest = U[:, :, 0:KP]

            def weight_parts(side):
                return split(wgt[side][:, :, 0:K], lambda n: wparts[:, :, 0:K, n + 1], rest[:, :, 0:K])

            weight_parts(DST).then_inc(wparts_ready, 1)

            def make(side, y, o, j, g):
                q0, q = FIRST[g] // 4, MSG_QUADS[g]
                for s, ids in enumerate((far[side], near[side])):
                    ins = dve.tensor_tensor(
                        oh[:, j, s, q0:q0 + q, :, :],
                        tile(ids, o)[:, :, 4 * q0:4 * (q0 + q)].rearrange("p a (q c) -> p (a q) c", c=4)
                        .unsqueeze(2).to_broadcast([P, q, P, 4]),
                        iota_4[:, :, :].unsqueeze(1).to_broadcast([P, q, P, 4]), ALU.is_equal)
                ins.then_inc(oh_made, 1)

            dve.wait_ge(iotas, 5)
            for g in range(NG):
                make(DST, 0, 0, 0, g)

            def makes(os):
                for o, j in os:
                    if j == 0 and len(os) == 1:
                        break
                    dve.wait_ge(tiles_full, AHEAD + NG * o)
                    for g in range(NG):
                        make(DST, o + 1, o + 1, 1 - j, g)

            in_pairs(dve, makes)
            dve.wait_ge(deg_read, AHEAD + T)
            dve.wait_ge(tiles_full, AHEAD + NG * T)
            dve.wait_ge(corrected, 1)
            link(dve.tensor_reduce(wsum[:, :], deg[:, :, 1:4], AX.X, ALU.add))
            link(dve.tensor_scalar(dinv[:, 0, :], wsum[:, :], 1.0, None, ALU.add))
            dve.tensor_scalar(stat[:, 1, :], dinv[:, 0, :], 1e-30, None, ALU.max).then_inc(sqrt_in, 1)
            root()
            link(dve.scalar_tensor_tensor(out=dinv[:, 0, :], in0=dinv[:, 0, :], scalar=0.0, in1=stat[:, 3, :],
                                          op0=ALU.is_gt, op1=ALU.mult))
            dve.tensor_scalar(stat[:, 1, :], deg[:, :, 0], 1.0, 1.0, ALU.add, ALU.max).then_inc(sqrt_in, 1)
            root()
            link(dve.tensor_copy(dinv[:, 1, :], stat[:, 3, :]))
            link(dve.tensor_scalar(icnt[:, 0, :], deg[:, :, 0], 1.0, None, ALU.max))
            link(dve.reciprocal(icnt[:, 0, :], icnt[:, 0, :]))
            dve.wait_ge(nodes_in, 32)
            dve.wait_ge(weights_in, WEIGHTS)
            link(dve.tensor_tensor(bias[:, 1, :], bias[:, 1, :], bias[:, 6, :], ALU.add))

            weighted = counted_layers = 0
            dve.sem_inc(gathered, AHEAD)
            for l in range(5):
                if l < 4:
                    normed(X[:, :, :])
                    link(dve.scalar_tensor_tensor(out=H[:, :, :], in0=V[:, :, :], scalar=0.0, in1=rows(stat[:, 3, :]),
                                                  op0=ALU.max, op1=ALU.mult))
                sent = H
                if l < 2:
                    link(dve.tensor_tensor(V[:, :, :], H[:, :, :], rows(dinv[:, l, :]), ALU.mult))
                    sent = V
                split(sent[:, :, :], lambda n: parts[:, :, n, :], U[:, :, :]).then_inc(parts_ready, 1)
                if l in WEIGHTED:
                    side = WEIGHTED[l]
                    if l == 2:
                        weight_parts(side).then_inc(wparts_ready, 1)
                    y = (weighted + 1) * T
                    for g in range(NG):
                        make(side, y, 0, 0, g)

                    def messages(os):
                        for o, j in os:
                            m = weighted * T + o
                            for g in range(NG):
                                n = m * NG + g
                                w = min(K, FIRST[g + 1]) - FIRST[g]
                                dve.wait_ge(gathered, AHEAD + n + 1)
                                dve.wait_ge(summed, AHEAD + n - 1)
                                dve.tensor_tensor(msg[:, g % 2, 0:w, :],
                                                  gat[g % 2][:, 0:w * F].rearrange("p (c f) -> p c f", f=F),
                                                  tile(wgt[side], o)[:, :, FIRST[g]:FIRST[g] + w].rearrange("p a k -> p (a k)")
                                                  .unsqueeze(2).to_broadcast([P, w, F]), ALU.mult).then_inc(msg_ready, 1)
                                if len(os) == 2:
                                    if g == 0:
                                        dve.wait_ge(summed, AHEAD + m * NG)
                                    make(side, y + 1 + o, o + 1, 1 - j, g)

                    in_pairs(dve, messages)
                    weighted += 1
                    dve.wait_ge(agg_ready, AHEAD + weighted * T)
                else:
                    with dve.Fori(0, T // RING) as it:
                        for r in range(RING):
                            m = counted_layers * T + RING * it + r
                            dve.wait_ge(counted, AHEAD + m + 1)
                            dve.tensor_reduce(tile(agg, RING * it + r)[:, :, 0:F].rearrange("p a f -> p (a f)"),
                                              acc[r % 2][:, 0:3 * F].rearrange("p (x f) -> p f x", x=3),
                                              AX.X, ALU.add).then_inc(counts_read, 1)
                    counted_layers += 1
                    dve.wait_ge(counts_read, AHEAD + counted_layers * T)
                dve.wait_ge(corrected, l + 2)
                if l < 2:
                    link(dve.tensor_tensor(U[:, :, :], agg[:, :, 0:F], V[:, :, :], ALU.add))
                    dve.tensor_tensor(TH[:, :, 0:F], U[:, :, :], rows(dinv[:, l, :]), ALU.mult).then_inc(th_ready, 1)
                elif l == 2:
                    link(dve.tensor_reduce(gsum[:, :], agg[:, :, F + 1:F + 4], AX.X, ALU.add))
                    link(dve.tensor_scalar(icnt[:, 1, :], agg[:, :, F], 1.0, None, ALU.max))
                    link(dve.reciprocal(icnt[:, 1, :], icnt[:, 1, :]))
                    dve.tensor_tensor(TH[:, :, F], gsum[:, :], icnt[:, 1, :], ALU.mult)
                    dve.tensor_tensor(TH[:, :, 0:F], agg[:, :, 0:F], rows(icnt[:, 1, :]), ALU.mult).then_inc(th_ready, 1)
                else:
                    dve.tensor_tensor(TH[:, :, 0:F], agg[:, :, 0:F], rows(icnt[:, 0, :]), ALU.mult).then_inc(th_ready, 1)
                for q in range(NQ):
                    n = NQ * l + q
                    a, b = 4 * q, min(T, 4 * q + 4)
                    dve.wait_ge(projected, n + 1)
                    came = proj[n % 2][:, 0:(b - a) * F].rearrange("p (t f) -> p t f", f=F)
                    if l == 2:
                        ins = dve.tensor_copy(U[:, a:b, :], came)
                    else:
                        ins = dve.tensor_tensor(U[:, a:b, :], came,
                                                bias[:, {0: 0, 1: 1, 3: 2, 4: 3}[l], :].unsqueeze(1).to_broadcast([P, b - a, F]),
                                                ALU.add)
                    ins.then_inc(proj_read, 1)
                dve.wait_ge(proj_read, NQ * (l + 1))
                if l == 0:
                    normed(U[:, :, :])
                    link(dve.tensor_tensor(V[:, :, :], V[:, :, :], rows(stat[:, 3, :]), ALU.mult))
                    link(dve.tensor_tensor(V[:, :, :], V[:, :, :], bias[:, 4, :].unsqueeze(1).to_broadcast([P, T, F]), ALU.mult))
                    dve.tensor_tensor(V[:, :, :], V[:, :, :], bias[:, 5, :].unsqueeze(1).to_broadcast([P, T, F]),
                                      ALU.add).then_inc(gelu_in, 1)
                    dve.wait_ge(gelu_out, 1)
                if l == 3:
                    link(dve.tensor_scalar(H[:, :, :], U[:, :, :], 0.0, None, ALU.max))
                elif l < 4:
                    link(dve.tensor_tensor(X[:, :, :], X[:, :, :], U[:, :, :], ALU.add))
                else:
                    dve.tensor_tensor(X[:, :, :], X[:, :, :], U[:, :, :], ALU.add).then_inc(result, 1)

        @block.tensor
        def _(pe):
            pe.sem_inc(tiles_full, AHEAD)
            pe.sem_inc(tiles_read, AHEAD)
            pe.sem_inc(deg_read, AHEAD)
            pe.sem_inc(agg_ready, AHEAD)
            pe.sem_inc(summed, AHEAD)
            pe.sem_inc(gat_ready, AHEAD)
            pe.sem_inc(msg_ready, AHEAD)
            pe.sem_inc(counted, AHEAD)
            pe.sem_inc(counts_read, AHEAD)
            pe.wait_ge(consts, 1)
            for a in range(2):
                for lo, hi in ((0, 512), (512, B)):
                    pe.matmul(counts[a][:, lo // 512, 0:hi - lo], ones[:, :], onehot[:, G - 1, lo:hi], start=True, stop=True,
                              skip_group_check=True)

            def count(a, left, v):
                for lo, hi in ((0, 512), (512, B)):
                    ins = pe.matmul(counts[a][:, lo // 512, 0:hi - lo], left[:, :], onehot[:, v % G, lo:hi],
                                    start=False, stop=True, skip_group_check=True)
                return ins

            with pe.Fori(0, GROUPS // 2) as it:
                for v in range(2 * G):
                    pe.wait_ge(rank_read, 2 * G * it + v + 1)
                    count(v % 2, after, v - 2)
                    count(v % 2, ones, v - 1)
                    pe.wait_ge(oh_ready, 2 * G * it + v + 1)
                    count(v % 2, before, v).then_inc(rank_ready, 1)

            pe.wait_ge(left_counted, 1)
            pe.matmul(acc[0][:, 0:1], ones[:, :], left_b[:, :], start=True, stop=True).then_inc(left_summed, 1)
            pe.wait_ge(weights_in, WEIGHTS)
            pe.transpose(acc[1][0:F, 0:F], wn[:, :], ident_f[0:F, 0:F]).then_inc(wn_turned, 1)
            pe.wait_ge(wn_ready, 1)
            pe.wait_ge(wparts_ready, 1)

            def count_tiles(os):
                for o, j in os:
                    for g in range(NG):
                        n = o * NG + g
                        pe.wait_ge(oh_made, n + 1)
                        pe.wait_ge(tiles_read, AHEAD + n - 1)
                        if g == 0:
                            pe.wait_ge(deg_read, AHEAD + o - 1)
                        for k in range(FIRST[g], min(K, FIRST[g + 1])):
                            t = k // 2 - FIRST[g] // 2
                            rows_n = oh[:, j, 1, k // 4, :, k % 4]
                            pe.matmul(tiles[g % 2][:, t * P:(t + 1) * P], oh[:, j, 0, k // 4, :, k % 4], rows_n,
                                      start=(k % 2 == 0), stop=(k % 2 == 1 or k == K - 1))
                            ins = pe.matmul(acc[j][:, 0:4], rows_n, tile(wparts, o)[:, :, k, :].rearrange("p a w -> p (a w)"),
                                            start=(k == 0), stop=(k == K - 1))
                        ins.then_inc(tiles_full, 1)

            in_pairs(pe, count_tiles)

            weighted = counted_layers = 0
            for l in range(5):
                pe.wait_ge(parts_ready, l + 1)
                if l in WEIGHTED:
                    side = WEIGHTED[l]
                    pe.wait_ge(wparts_ready, weighted + 1)

                    def turn_oh(m, o, j, g):
                        n = m * NG + g
                        pe.wait_ge(oh_made, (T + m) * NG + g + 1)
                        pe.wait_ge(gat_ready, AHEAD + n - 1)
                        for k in range(FIRST[g], min(K, FIRST[g + 1])):
                            c = k - FIRST[g]
                            ins = pe.transpose(turned_oh[g % 2][:, c * P:(c + 1) * P], oh[:, j, 0, k // 4, :, k % 4], ident_h[:, :])
                        ins.then_inc(oh_turned, 1)

                    def gather(m, o, j, g):
                        n = m * NG + g
                        pe.wait_ge(gat_ready, AHEAD + n + 1)
                        pe.wait_ge(msg_ready, AHEAD + n - 1)
                        for k in range(FIRST[g], min(K, FIRST[g + 1])):
                            c = k - FIRST[g]
                            for part in range(3):
                                here = parts[:, k // 2, part, :] if k < 2 * T else tile(parts, o)[:, :, part, :].rearrange("p a f -> p (a f)")
                                ins = pe.matmul(gat[g % 2][:, c * F:(c + 1) * F], gat_t[:, g % 2, c * P:(c + 1) * P], here,
                                                start=(part == 0), stop=(part == 2))
                        ins.then_inc(gathered, 1)

                    def sum_up(m, o, j, g):
                        n = m * NG + g
                        pe.wait_ge(msg_ready, AHEAD + n + 1)
                        pe.wait_ge(sum_ready, n + 1)
                        if g == 0:
                            pe.wait_ge(agg_ready, AHEAD + m - 1)
                        for k in range(FIRST[g], min(K, FIRST[g + 1])):
                            c = k - FIRST[g]
                            ins = pe.matmul(acc[j][:, 0:F], sum_f[:, g % 2, c * P:(c + 1) * P], msg[:, g % 2, c, :],
                                            start=(k == 0), stop=(k == K - 1), skip_group_check=(l == 2))
                            if l == 2:
                                ins = pe.matmul(acc[j][:, F:F + 4], oh[:, j, 1, k // 4, :, k % 4],
                                                tile(wparts, o)[:, :, k, :].rearrange("p a w -> p (a w)"),
                                                start=False, stop=(k == K - 1), skip_group_check=True)
                        ins.then_inc(summed, 1)

                    def chunks(os):
                        todo = [(weighted * T + o, o, j, g) for o, j in os for g in range(NG)]
                        turn_oh(*todo[0])
                        for i, at in enumerate(todo):
                            if i + 1 < len(todo):
                                turn_oh(*todo[i + 1])
                            gather(*at)
                            if i:
                                sum_up(*todo[i - 1])
                        sum_up(*todo[-1])

                    in_pairs(pe, chunks)
                    weighted += 1
                else:
                    with pe.Fori(0, T // RING) as it:
                        for r in range(RING):
                            o = RING * it + r
                            m = counted_layers * T + o
                            pe.wait_ge(counts_in[r], 16 * (counted_layers * (T // RING) + it + 1))
                            pe.wait_ge(counts_read, AHEAD + (m - 1 if r else m))
                            for t in range(TC):
                                here = (parts[:, t, :, :] if t < T else tile(parts, o).rearrange("p a x f -> p (a x) f"))
                                ins = pe.matmul(acc[r % 2][:, 0:3 * F], cnt_in[:, r, t * P:(t + 1) * P],
                                                here.rearrange("p x f -> p (x f)"), start=(t == 0), stop=(t == TC - 1))
                            ins.then_inc(counted, 1)
                    counted_layers += 1

                pe.wait_ge(th_ready, l + 1)

                def turns(q):
                    n = NQ * l + q
                    if n >= 2:
                        pe.wait_ge(tht_ready, n - 1)
                    for t in range(4 * q, min(T, 4 * q + 4)):
                        ins = pe.transpose(turn[n % 2][:, t % 4 * P:(t % 4 + 1) * P], TH[:, t, :], ident_f[:, :])
                    ins.then_inc(turned, 1)

                turns(0)
                for q in range(NQ):
                    n = NQ * l + q
                    if q + 1 < NQ:
                        turns(q + 1)
                    pe.wait_ge(tht_ready, n + 1)
                    if n >= 2:
                        pe.wait_ge(proj_read, n - 1)
                    for t in range(4 * q, min(T, 4 * q + 4)):
                        ins = pe.matmul(proj[n % 2][:, t % 4 * F:(t % 4 + 1) * F], tht[:, n % 2, t % 4 * P:(t % 4 + 1) * P],
                                        WS[:, l, :], start=True, stop=True)
                    ins.then_inc(projected, 1)


_INS = ["x", "src", "dst", "edge_attr_16", "edge_weight1", "L0_gnn_W", "L0_gnn_b", "L0_gnn_gamma", "L0_gnn_beta",
        "L1_gnn_W", "L1_gnn_b", "L1_gnn_W_lin", "L1_gnn_b_lin", "L2_gnn_W_edge", "L2_gnn_b_edge", "L2_gnn_W_node",
        "L2_gnn_b_node", "L3_gnn_w1_l", "L3_gnn_b1", "L3_gnn_w1_r", "L3_gnn_w2_l", "L3_gnn_b2", "L3_gnn_w2_r"]


def kernel(**inputs):
    import numpy as _np
    import concourse.bacc as _bacc
    from concourse.bass_utils import run_bass_kernel_spmd as _run

    nc = _bacc.Bacc("TRN2", target_bir_lowering=False, num_devices=1)
    arrays, args = {}, []
    for name in _INS:
        a = _np.ascontiguousarray(inputs[name])
        arrays[f"in_{name}"] = a
        args.append(nc.dram_tensor(f"in_{name}", a.shape, mybir.dt.from_np(a.dtype), kind="ExternalInput").ap())
    args.append(nc.dram_tensor("out", (N, F), f32, kind="ExternalOutput").ap())
    args.append(nc.dram_tensor("slots", (ROWS, 4), f32).ap())
    args.append(nc.dram_tensor("count_table", (T, P, TC * P), bf16).ap())
    args.append(nc.dram_tensor("rows_table", (T * P + 1, F), f32).ap())
    args.append(nc.dram_tensor("added_table", (T * P + 1, F + 2), f32).ap())
    args.append(nc.dram_tensor("marks_table", (2, P, C), i32).ap())
    args.append(nc.dram_tensor("fields_table", (P * C, 4), f32).ap())
    gnn(nc, *args)
    return _run(nc, [arrays], core_ids=[0]).results[0]["out"]
```

```python
import concourse.bass as bass
from concourse import mybir
from contextlib import ExitStack

N = 3125
F = 64
E = 103125
EDGE_F = 16
P = 128
T = -(-N // P)
TAIL = N - (T - 1) * P
C = -(-E // P)
E_TAIL = E - (P - 1) * C
B = T * T
HALF = P
ROWS2 = 2 * HALF * B
ROWS = ROWS2 + HALF * T
CH = 2 * B + T
G = 13
GROUPS = C // G
assert GROUPS * G == C and GROUPS % 2 == 0
K = 2 * T + 1
QUADS = -(-K // 4)
KP = 4 * QUADS
MSG_QUADS = [2, 2, 2, 2, 1, 2, 1, 1]
assert sum(MSG_QUADS) == QUADS
NG = len(MSG_QUADS)
FIRST = [4 * sum(MSG_QUADS[:g]) for g in range(NG + 1)]
SPLIT = (1, 3, 5, 7)
PLAIN = [g for g in range(NG) if g not in SPLIT]
assert all(g % 4 in (0, 2) for g in PLAIN)
TC = T + 1
AHEAD = 2 * NG
RING = 5
assert T % RING == 0 and T % 2 == 1
FAR = 1.0e6
EPS = 1e-5

f32, bf16, f16, i32 = mybir.dt.float32, mybir.dt.bfloat16, mybir.dt.float16, mybir.dt.int32
ALU = mybir.AluOpType
ACT = mybir.ActivationFunctionType
AX = mybir.AxisListType



def gnn(nc, x, src, dst, edge_attr, edge_w, w0, b0, gamma, beta, w1, b1, wlin, blin,
        wedge, bedge, wnode, bnode, w3l, b3, w3r, w4l, b4, w4r, out, slots, count_table, rows_table, added_table,
        marks_table, fields_table):
    ctx = ExitStack()
    with ctx:
        def sb(name, shape, dt=f32):
            return ctx.enter_context(nc.sbuf_tensor(name, shape, dt))

        def sem(name):
            return ctx.enter_context(nc.semaphore(name))

        src_i = sb("src_i", [P, C], i32)
        dst_i = sb("dst_i", [P, C], i32)
        payload = sb("payload", [P, C, 4])
        work = sb("work", [P, 6 * C + 1])
        w_in, src_t, dst_t, third, rank = [work[:, n * C:(n + 1) * C] for n in range(5)]
        key = work[:, 5 * C:6 * C + 1]
        sum_f = work[:, 0:2 * 1024].rearrange("p (r e) -> p r e", r=2)
        gat_t = work[:, 2048:2048 + 1024].bitcast(bf16).rearrange("p (r e) -> p r e", r=2)
        split_msg = work[:, 3072:3072 + 1536].bitcast(bf16).rearrange("p (r n c f) -> p r n c f", r=2, n=3, f=F)
        tht = work[:, 0:2 * 4 * P].rearrange("p (r e) -> p r e", r=2)
        iota_b = sb("iota_b", [P, B], f16)
        sorting = sb("sorting", [P, G * B + 1], bf16)
        onehot = sorting[:, 0:G * B].rearrange("p (a b) -> p a b", a=G)
        TH = sorting[:, 0:2 * T * 2 * F].bitcast(f32).rearrange("p (t f) -> p t f", t=T)
        scratch = sb("scratch", [P, 2 * B], bf16)
        junk = scratch[:, :].rearrange("p (r b) -> p r b", r=2)
        added_rows = TH[:, :, 0:F]
        added_sums = scratch[:, 0:4 * T].bitcast(f32).rearrange("p (t f) -> p t f", f=2)
        edge_row = sb("edge_row", [1, F + 2])
        edge_dst = sb("edge_dst", [1, 1], i32)
        left_over = sb("left_over", [P, 1])
        left_b = sb("left_b", [P, 1], bf16)
        left_i = sb("left_i", [P, 1], i32)
        before = sb("before", [P, P], bf16)
        after = sb("after", [P, P], bf16)
        ones = sb("ones", [P, P], bf16)
        pos = sb("pos", [P, 4, G])
        place = sb("place", [P, 2, G], i32)
        pay = sb("pay", [P, 2, G, 4])
        slot = sb("slot", [P, CH, 4])
        cnt_out = slot[:, :, :].rearrange("p c f -> p (c f)")[:, 0:TC * P].bitcast(bf16).rearrange(
            "p (r n) -> p r n", r=2)
        PW = F + 2
        msg = [slot[:, :, :].rearrange("p c f -> p (c f)")[:, TC * P + 8 * PW * n:TC * P + 8 * PW * (n + 1)] for n in range(3)]
        plain_msg = {n: msg[n].rearrange("p (c f) -> p c f", f=PW) for n in (0, 2)}
        assert TC * P + 3 * 8 * PW <= 4 * CH
        near = [sb("near_src", [P, T, KP], bf16), sb("near_dst", [P, T, KP], bf16)]
        far = [sb("far_src", [P, T, KP], bf16), sb("far_dst", [P, T, KP], bf16)]
        wgt = [sb("wgt_src", [P, T, KP]), sb("wgt_dst", [P, T, KP])]
        wparts = sb("wparts", [P, T, KP, 4], bf16)
        iota_f = sb("iota_f", [P, P], f16)
        iota_4 = sb("iota_4", [P, P, 4], bf16)
        iota_p = sb("iota_p", [P, 1])
        ident_h = sb("ident_h", [P, P], bf16)
        ident_f = sb("ident_f", [P, P])
        OH = QUADS * P * 4
        big = sb("big", [P, 2 * OH])
        attr = big[:, 0:C * EDGE_F].rearrange("p (c f) -> p c f", f=EDGE_F)
        oh = big[:, :].bitcast(bf16).rearrange("p (r s q l c) -> p r s q l c", r=2, s=2, q=QUADS, c=4)
        cnt_in = big[:, 0:RING * TC * P // 2].bitcast(bf16).rearrange("p (r n) -> p r n", r=RING)
        X = sb("X", [P, T, F])
        H = TH[:, :, F:2 * F]
        V = sb("V", [P, T, F])
        U = sb("U", [P, T, F])
        msg.append(U[:, :, :].rearrange("p t f -> p (t f)")[:, 0:512])
        marks = U[:, :, :].rearrange("p t f -> p (t f)")[0:1, 0:C].bitcast(i32)
        agg = sb("agg", [P, T, F + 6])
        sq = agg[:, :, 0:F]
        tmp_i = agg[:, :, :].rearrange("p t f -> p (t f)")[:, 0:C].bitcast(i32)
        parts = sb("parts", [P, T, 3, F], bf16)
        stat = sb("stat", [P, 4, T])
        deg = sb("deg", [P, T, 4])
        wsum = sb("wsum", [P, T])
        gsum = sb("gsum", [P, T])
        dinv = sb("dinv", [P, 2, T])
        icnt = sb("icnt", [P, 2, T])
        wedge_b = sb("wedge_b", [P, EDGE_F])
        bedge_b = sb("bedge_b", [P, 1])
        WS = sb("WS", [P, 5, F])
        bias = sb("bias", [P, 7, F])
        wn = sb("wn", [F, F])

        counts = [ctx.enter_context(nc.psum_tensor(f"counts{a}", [P, 2, 512], f32)) for a in range(2)]
        turned_oh = [ctx.enter_context(nc.psum_tensor(f"turned_oh{a}", [P, 1024], bf16)) for a in range(2)]
        acc = [ctx.enter_context(nc.psum_tensor(f"acc{a}", [P, 512], f32)) for a in range(2)]
        tiles = gat = turn = [counts[0][:, 0, :], counts[0][:, 1, :]]
        proj = [counts[1][:, 0, :], counts[1][:, 1, :]]

        cleared = sem("cleared")
        nodes_cleared = sem("nodes_cleared")
        edges_in = sem("edges_in")
        attrs_in = sem("attrs_in")
        small_in = sem("small_in")
        nodes_in = sem("nodes_in")
        centred = sem("centred")
        squared = sem("squared")
        sent_ready = sem("sent_ready")
        nodes_high = sem("nodes_high")
        nodes_rest = sem("nodes_rest")
        nodes_middle = sem("nodes_middle")
        weights_in = sem("weights_in")
        iotas = sem("iotas")
        consts = sem("consts")
        dve_step = sem("dve_step")
        gate_sum = sem("gate_sum")
        gates = sem("gates")
        payloads = sem("payloads")
        oh_ready = sem("oh_ready")
        rank_ready = sem("rank_ready")
        rank_read = sem("rank_read")
        placed = sem("placed")
        place_step = sem("place_step")
        wparts_ready = sem("wparts_ready")
        oh_made = sem("oh_made")
        paid = sem("paid")
        scattered = [sem("scattered0"), sem("scattered1")]
        sorted_in = sem("sorted_in")
        left_counted = sem("left_counted")
        left_summed = sem("left_summed")
        left_known = sem("left_known")
        corrected = sem("corrected")
        fix_step = sem("fix_step")
        fix_moved = sem("fix_moved")
        edge_in = sem("edge_in")
        marks_in = sem("marks_in")
        dst_in = sem("dst_in")
        edge_scaled = sem("edge_scaled")
        edge_added = sem("edge_added")
        tiles_full = sem("tiles_full")
        tiles_read = sem("tiles_read")
        block_out = sem("block_out")
        block_sent = sem("block_sent")
        counted = sem("counted")
        counts_read = sem("counts_read")
        counts_in = [sem(f"counts_in{r}") for r in range(RING)]
        deg_read = sem("deg_read")
        parts_ready = sem("parts_ready")
        oh_turned = sem("oh_turned")
        gat_ready = sem("gat_ready")
        sum_ready = sem("sum_ready")
        gathered = sem("gathered")
        msg_ready = sem("msg_ready")
        high_made = sem("high_made")
        rest_made = sem("rest_made")
        middle_made = sem("middle_made")
        split_ready = sem("split_ready")
        summed = sem("summed")
        agg_ready = sem("agg_ready")
        th_ready = sem("th_ready")
        turned = sem("turned")
        tht_ready = sem("tht_ready")
        projected = sem("projected")
        proj_read = sem("proj_read")
        sqrt_in = sem("sqrt_in")
        sqrt_out = sem("sqrt_out")
        gelu_in = sem("gelu_in")
        gelu_out = sem("gelu_out")
        wn_turned = sem("wn_turned")
        wn_ready = sem("wn_ready")
        result = sem("result")
        stored = sem("stored")

        PRESET = 1
        SRC, DST = 0, 1
        WEIGHTED = {0: DST, 2: SRC}
        COUNTED = (1, 3, 4)
        HALVES = ((0, T // 2), (T // 2, T))
        NQ = -(-T // 4)

        def slot_parts():
            yield (slot[:, 0:2 * B, :].rearrange("p (q b) f -> p q (b f)", q=2),
                   slots[0:ROWS2, :].rearrange("(q p b) f -> p q (b f)", q=2, p=P))
            yield (slot[:, 2 * B:CH, :].rearrange("p b f -> p (b f)"),
                   slots[ROWS2:ROWS, :].rearrange("(p b) f -> p (b f)", p=P))

        def in_pairs(eng, body):
            with eng.Fori(0, T // 2) as it:
                body([(2 * it, 0), (2 * it + 1, 1)])
            body([(T - 1, 0)])

        def flow(eng, *stages):
            def one_tile(o, j, first=False):
                for g in range(NG):
                    for lag, f in stages:
                        tiles_back = -((g - lag) // NG)
                        if not (first and tiles_back):
                            f(o - tiles_back, (j + tiles_back) % 2, (g - lag) % NG)

            one_tile(0, 0, first=True)
            with eng.Fori(0, T // 2) as it:
                one_tile(2 * it + 1, 1)
                one_tile(2 * it + 2, 0)
            for g in range(max(lag for lag, f in stages)):
                for lag, f in stages:
                    if g < lag:
                        f(T - 1, 0, NG + g - lag)

        def tile(ap, o):
            return ap[:, bass.ds(o, 1)]

        block = ctx.enter_context(nc.Block())

        @block.sync
        def _(sp):
            m = (P - 1) * C
            sp.wait_ge(cleared, 1)
            for ap, to in ((src, src_i), (dst, dst_i)):
                sp.dma_start(to[0:P - 1, :], ap[0:m].rearrange("(p c) -> p c", p=P - 1)).then_inc(edges_in, 16)
                sp.dma_start(to[P - 1:P, 0:E_TAIL], ap[m:E].rearrange("(a c) -> a c", a=1)).then_inc(edges_in, 16)
            sp.dma_start(attr[0:P - 1, :, :], edge_attr[0:m, :].rearrange("(p c) f -> p c f", p=P - 1)).then_inc(attrs_in, 16)
            sp.dma_start(attr[P - 1:P, 0:E_TAIL, :], edge_attr[m:E, :].rearrange("(p c) f -> p c f", p=1)).then_inc(attrs_in, 16)
            sp.dma_start(w_in[0:P - 1, :], edge_w[0:m, :].rearrange("(p c) a -> p (c a)", p=P - 1)).then_inc(edges_in, 16)
            sp.dma_start(w_in[P - 1:P, 0:E_TAIL], edge_w[m:E, :].rearrange("(p c) a -> p (c a)", p=1)).then_inc(edges_in, 16)
            sp.wait_ge(nodes_cleared, 1)
            sp.dma_start(X[:, 0:T - 1, :], x[0:(T - 1) * P, :].rearrange("(t p) f -> p t f", p=P)).then_inc(nodes_in, 16)
            sp.dma_start(X[0:TAIL, T - 1, :], x[(T - 1) * P:N, :]).then_inc(nodes_in, 16)
            for l, (top, bottom) in enumerate(((w0, None), (w1, wlin), (None, None), (w3l, w3r), (w4l, w4r))):
                if top is not None:
                    sp.dma_start(WS[0:F, l, :], top).then_inc(weights_in, 16)
                if bottom is not None:
                    sp.dma_start(WS[F:2 * F, l, :], bottom).then_inc(weights_in, 16)
            sp.dma_start(wn[:, :], wnode).then_inc(weights_in, 16)
            sp.dma_start(WS[F:F + 1, 2, :], bnode.rearrange("(a n) -> a n", a=1)).then_inc(weights_in, 16)
            for n, ap in enumerate((b0, b1, b3, b4, gamma, beta, blin)):
                sp.dma_start(bias[:, n, :], ap.rearrange("(a n) -> a n", a=1).to_broadcast([P, F])).then_inc(weights_in, 16)
            for s in range(2):
                sp.wait_ge(scattered[s], 16 + 16 * G * (GROUPS // 2))
            for here, there in slot_parts():
                sp.dma_start(here, there).then_inc(sorted_in, 16)

            def send(os):
                for o, j in os:
                    sp.wait_ge(tiles_read, AHEAD + NG * (o + 1))
                    sp.dma_start(count_table[bass.ds(o, 1), :, :].rearrange("a p n -> p (a n)"),
                                 cnt_out[:, j, :]).then_inc(block_out, 16)
                    sp.wait_ge(block_out, 16 * (o + 1))
                    sp.sem_inc(block_sent, 1)

            in_pairs(sp, send)
            for n, l in enumerate(COUNTED):
                sp.wait_ge(parts_ready, l + 1)
                with sp.Fori(0, T // RING) as it:
                    for r in range(RING):
                        sp.wait_ge(counted, AHEAD + n * T + RING * it + r - RING + 1)
                        sp.dma_start(cnt_in[:, r, :],
                                     count_table[bass.ds(it * RING + r, 1), :, :].rearrange("a p n -> p (a n)"))\
                          .then_inc(counts_in[r], 16)
            sp.wait_ge(result, NQ // 2)
            t = 4 * (NQ // 2)
            sp.dma_start(out[0:t * P, :].rearrange("(t p) f -> p t f", p=P), X[:, 0:t, :]).then_inc(stored, 16)
            sp.wait_ge(result, NQ)
            sp.dma_start(out[t * P:(T - 1) * P, :].rearrange("(t p) f -> p t f", p=P), X[:, t:T - 1, :]).then_inc(stored, 16)
            sp.dma_start(out[(T - 1) * P:N, :], X[0:TAIL, T - 1, :]).then_inc(stored, 16)
            sp.wait_ge(stored, 48)

        WEIGHTS = 16 * (7 + 2 + 7)

        @block.gpsimd
        def _(pool):
            pool.iota(tmp_i[:, :], [[1, C]], base=0, channel_multiplier=C).then_inc(iotas, 1)
            pool.iota(iota_f[:, :], [[1, P]], base=0, channel_multiplier=0,
                      allow_small_or_imprecise_dtypes=True).then_inc(iotas, 1)
            pool.iota(iota_p[:, :], [[0, 1]], base=0, channel_multiplier=1,
                      allow_small_or_imprecise_dtypes=True).then_inc(iotas, 1)
            pool.iota(iota_b[:, :], [[1, B]], base=0, channel_multiplier=0,
                      allow_small_or_imprecise_dtypes=True).then_inc(iotas, 1)
            pool.iota(iota_4[:, :, :], [[1, P], [0, 4]], base=0, channel_multiplier=0,
                      allow_small_or_imprecise_dtypes=True).then_inc(iotas, 1)
            pool.memset(slot[:, :, 0:2], -1.0).then_inc(iotas, 1)
            pool.memset(slot[:, :, 2:4], 0.0).then_inc(iotas, 1)
            pool.wait_ge(iotas, 7)
            for s, (here, there) in enumerate(slot_parts()):
                pool.dma_start(there, here).then_inc(scattered[s], 16)
            for side in range(2):
                pool.memset(near[side][:, :, :], -1.0)
                pool.memset(far[side][:, :, :], -1.0)
            pool.memset(WS[:, :, :], 0.0)
            pool.memset(X[:, :, :], 0.0).then_inc(nodes_cleared, 1)
            pool.wait_ge(scattered[0], 16)
            pool.wait_ge(scattered[1], 16)
            last_row = pool.to_reg(ROWS - 1)
            group = pool.alloc_register("group")
            pool.reg_mov(group, 1)
            with pool.Fori(0, GROUPS // 2) as it:
                for s in range(2):
                    pool.reg_add(group, group, 1)
                    pool.wait_ge(iotas, 7)
                    pool.wait_ge(placed, group)
                    pool.wait_ge(paid, group)
                    for u in range(G):
                        pool.indirect_dma_start(slots, bass.IndirectOffsetOnAxis(ap=place[:, s, u:u + 1], axis=0),
                                                pay[:, s, u, :], None, bounds_check=last_row,
                                                oob_is_err=False).then_inc(scattered[s], 16)

            pool.wait_ge(left_known, 1)
            left = pool.value_load(left_i[0:1, 0:1])
            steps, moves = [0], [0]

            def link(ins):
                steps[0] += 1
                ins.then_inc(fix_step, 1)
                pool.wait_ge(fix_step, steps[0])

            def move(to, here, **how):
                moves[0] += 1
                pool.dma_start(to, here, **how).then_inc(fix_moved, 16)
                pool.wait_ge(fix_moved, 16 * moves[0])

            def again(*sems):
                for one in sems:
                    pool.dma_reset(range(one.num, one.num + 1))
                for one in sems:
                    pool.sem_clear(one)

            def by_tile(table):
                return table[1:T * P + 1, :].rearrange("(t p) f -> p t f", p=P)

            def add_edges(side, weight, rows):
                link(pool.memset(edge_row[:, :], 1.0))
                link(pool.memset(added_rows, 0.0))
                link(pool.memset(added_sums, 0.0))
                move(by_tile(added_table[:, 0:F]), added_rows)
                move(by_tile(added_table[:, F:F + 2]), added_sums)
                if rows is not None:
                    move(by_tile(rows_table), rows)
                with pool.Fori(0, P) as p:
                    pool.dma_start(marks, marks_table[0, bass.ds(p, 1), :]).then_inc(marks_in, 16)
                    pool.wait_ge(marks_in, 16)
                    again(marks_in)
                    with pool.Fori(0, C) as c:
                        marked = pool.value_load(marks[0:1, bass.ds(c, 1)], min_val=0, max_val=N)
                        with pool.If(marked > 0):
                            pool.dma_start(edge_dst[:, :], marks_table[1, bass.ds(p, 1), bass.ds(c, 1)]).then_inc(dst_in, 16)
                            pool.wait_ge(dst_in, 16)
                            ends = pool.value_load(edge_dst[0:1, 0:1], min_val=1, max_val=N)
                            there, here = (marked, ends) if side == DST else (ends, marked)
                            pool.dma_start(edge_row[0:1, F + 1:F + 2],
                                           fields_table[bass.ds(p * C + c, 1), weight:weight + 1]).then_inc(edge_in, 16)
                            if rows is not None:
                                pool.dma_start(edge_row[0:1, 0:F], rows_table[bass.ds(there, 1), :]).then_inc(edge_in, 16)
                            pool.wait_ge(edge_in, 16 if rows is None else 32)
                            if l in WEIGHTED:
                                pool.tensor_tensor(edge_row[0:1, 0:F], edge_row[0:1, 0:F],
                                                   edge_row[0:1, F + 1:F + 2].to_broadcast([1, F]), ALU.mult)\
                                    .then_inc(edge_scaled, 1)
                                pool.wait_ge(edge_scaled, 1)
                            pool.dma_start(added_table[bass.ds(here, 1), :], edge_row[0:1, :],
                                           accum_op=ALU.add).then_inc(edge_added, 16)
                            pool.wait_ge(edge_added, 16)
                            again(dst_in, edge_in, edge_added)
                            pool.sem_clear(edge_scaled)
                move(added_rows, by_tile(added_table[:, 0:F]))
                move(added_sums, by_tile(added_table[:, F:F + 2]))

            l = None
            pool.wait_ge(deg_read, AHEAD + T)
            with pool.If(left > 0):
                move(marks_table[0, :, :], src_i[:, :])
                move(marks_table[1, :, :], dst_i[:, :])
                move(fields_table.rearrange("(p c) f -> p c f", p=P), payload[:, :, :])
                add_edges(DST, 2, None)
                link(pool.tensor_tensor(deg[:, :, 0:2], deg[:, :, 0:2], added_sums, ALU.add))
            pool.sem_inc(corrected, 1)
            weighted = counted_layers = 0
            for l in range(5):
                pool.wait_ge(parts_ready, l + 1)
                if l in WEIGHTED:
                    weighted += 1
                    pool.wait_ge(agg_ready, AHEAD + weighted * T)
                else:
                    counted_layers += 1
                    pool.wait_ge(counts_read, AHEAD + counted_layers * T)
                with pool.If(left > 0):
                    add_edges(WEIGHTED.get(l, DST), 3 if l == 2 else 2, V[:, :, :] if l < 2 else H)
                    link(pool.tensor_tensor(agg[:, :, 0:F], agg[:, :, 0:F], added_rows, ALU.add))
                    if l == 2:
                        link(pool.tensor_tensor(agg[:, :, F:F + 2], agg[:, :, F:F + 2], added_sums, ALU.add))
                pool.sem_inc(corrected, 1)

        @block.scalar
        def _(act):
            act.dma_start(wedge_b[:, :], wedge.rearrange("k a -> a k").to_broadcast([P, EDGE_F])).then_inc(small_in, 16)
            act.dma_start(bedge_b[:, :], bedge.rearrange("(a n) -> a n", a=1).to_broadcast([P, 1])).then_inc(small_in, 16)
            act.wait_ge(gate_sum, 1)
            act.wait_ge(small_in, 32)
            act.activation(payload[:, :, 3], third, ACT.Sigmoid, bias=bedge_b[:, 0:1]).then_inc(gates, 1)
            act.wait_ge(gates, 1)
            act.wait_ge(payloads, 1)
            act.sem_inc(paid, PRESET)
            with act.Fori(0, GROUPS // 2) as it:
                for s in range(2):
                    act.wait_ge(scattered[s], 16 + 16 * G * it)
                    act.copy(pay[:, s, :, :], payload[:, bass.ds((2 * it + s) * G, G), :]).then_inc(paid, 1)

            halves = [0]

            def squares():
                for lo, hi in HALVES:
                    halves[0] += 1
                    act.wait_ge(centred, halves[0])
                    act.activation(sq[:, lo:hi, :], V[:, lo:hi, :], ACT.Square).then_inc(squared, 1)

            def root(n):
                act.wait_ge(sqrt_in, n + 1)
                act.activation(stat[:, 2, :], stat[:, 1, :], ACT.Sqrt).then_inc(sqrt_out, 1)

            act.wait_ge(wn_turned, 1)
            act.copy(WS[0:F, 2, :], acc[1][0:F, 0:F]).then_inc(wn_ready, 1)
            squares()
            root(0)

            def block_part(o, j, g):
                n = o * NG + g
                lo, w = FIRST[g] // 2 * P, 2 * MSG_QUADS[g] * P
                act.wait_ge(tiles_full, AHEAD + n + 1)
                if g == 0:
                    act.wait_ge(block_sent, AHEAD + o - 1)
                act.copy(cnt_out[:, j, lo:lo + w], tiles[g % 2][:, 0:w]).then_inc(tiles_read, 1)
                if g == NG - 1:
                    act.copy(tile(deg, o), acc[j][:, 0:4]).then_inc(deg_read, 1)

            act.sem_inc(block_sent, AHEAD)
            flow(act, (0, block_part))
            root(1)
            root(2)
            weighted = 0
            for l in range(5):
                sent = V if l < 2 else H
                act.wait_ge(sent_ready, l + 1)
                for lo, hi in HALVES:
                    act.copy(parts[:, lo:hi, 0, :], sent[:, lo:hi, :]).then_inc(nodes_high, 1)
                for h, (lo, hi) in enumerate(HALVES):
                    act.wait_ge(nodes_rest, 2 * l + h + 1)
                    act.copy(parts[:, lo:hi, 1, :], U[:, lo:hi, :]).then_inc(nodes_middle, 1)
                if l in WEIGHTED:
                    def turned_copy(o, j, g):
                        n = (weighted * T + o) * NG + g
                        w = min(K, FIRST[g + 1]) - FIRST[g]
                        act.wait_ge(oh_turned, n + 1)
                        act.wait_ge(gathered, AHEAD + n - 1)
                        act.copy(gat_t[:, g % 2, 0:w * P], turned_oh[g % 2][:, 0:w * P]).then_inc(gat_ready, 1)

                    def summing_rows(o, j, g):
                        if g in SPLIT:
                            return
                        n = (weighted * T + o) * NG + g
                        q = MSG_QUADS[g]
                        act.wait_ge(oh_made, T * NG + n + 1)
                        act.wait_ge(summed, AHEAD + n - 3)
                        act.copy(sum_f[:, PLAIN.index(g) % 2, 0:4 * q * P].rearrange("p (q c l) -> p q c l", q=q, c=4),
                                 oh[:, j, 1, FIRST[g] // 4:FIRST[g] // 4 + q, :, :].rearrange("p q l c -> p q c l"))\
                           .then_inc(sum_ready, 1)

                    def high(o, j, g):
                        if g in SPLIT:
                            n = (weighted * T + o) * NG + g
                            w = min(K, FIRST[g + 1]) - FIRST[g]
                            act.wait_ge(msg_ready, AHEAD + n + 1)
                            act.wait_ge(summed, AHEAD + n - 3)
                            act.copy(split_msg[:, SPLIT.index(g) % 2, 0, 0:w, :].rearrange("p c f -> p (c f)"),
                                     msg[g % 4][:, 0:w * F]).then_inc(high_made, 1)

                    def middle(o, j, g):
                        if g in SPLIT:
                            w = min(K, FIRST[g + 1]) - FIRST[g]
                            act.wait_ge(rest_made, (weighted * T + o) * len(SPLIT) + SPLIT.index(g) + 1)
                            act.copy(split_msg[:, SPLIT.index(g) % 2, 1, 0:w, :].rearrange("p c f -> p (c f)"),
                                     msg[g % 4][:, 0:w * F]).then_inc(middle_made, 1)

                    flow(act, (2, turned_copy), (6, summing_rows), (5, middle), (4, high))
                    weighted += 1
                for q in range(NQ):
                    n = NQ * l + q
                    w = min(4, T - 4 * q) * P
                    act.wait_ge(turned, n + 1)
                    if n >= 2:
                        act.wait_ge(projected, n - 1)
                    act.copy(tht[:, n % 2, 0:w], turn[n % 2][:, 0:w]).then_inc(tht_ready, 1)
                if l == 0:
                    squares()
                    root(3)
                    act.wait_ge(gelu_in, 1)
                    act.activation(U[:, :, :], V[:, :, :], ACT.Gelu).then_inc(gelu_out, 1)
                if l < 3:
                    squares()
                    root(4 + l)

        @block.vector
        def _(dve):
            steps_done = [0]
            roots, squares = [0], [0]

            def link(ins):
                steps_done[0] += 1
                ins.then_inc(dve_step, 1)
                dve.wait_ge(dve_step, steps_done[0])

            def rows(ap, width=F):
                return ap.unsqueeze(2).to_broadcast([P, ap.shape[1], width])

            def root():
                roots[0] += 1
                dve.wait_ge(sqrt_out, roots[0])
                link(dve.reciprocal(stat[:, 3, :], stat[:, 2, :]))

            def normed(a, summed_up=False):
                if not summed_up:
                    link(dve.tensor_reduce(stat[:, 0, :], a, AX.X, ALU.add))
                link(dve.tensor_scalar(stat[:, 0, :], stat[:, 0, :], -1.0 / F, None, ALU.mult))
                for lo, hi in HALVES:
                    ins = dve.tensor_tensor(V[:, lo:hi, :], a[:, lo:hi, :], rows(stat[:, 0, lo:hi]), ALU.add)
                    ins.then_inc(centred, 1)
                for lo, hi in HALVES:
                    squares[0] += 1
                    dve.wait_ge(squared, squares[0])
                    ins = dve.tensor_reduce(stat[:, 1, lo:hi], sq[:, lo:hi, :], AX.X, ALU.add)
                link(ins)
                dve.tensor_scalar(stat[:, 1, :], stat[:, 1, :], 1.0 / F, EPS, ALU.mult, ALU.add).then_inc(sqrt_in, 1)
                root()

            def split(a, out, rest):
                link(dve.tensor_copy(out(0), a))
                link(dve.tensor_tensor(rest, a, out(0), ALU.subtract))
                link(dve.tensor_copy(out(1), rest))
                return dve.tensor_tensor(out(2), rest, out(1), ALU.subtract)

            dve.memset(src_i[:, E_TAIL:C], 0)
            dve.memset(dst_i[:, E_TAIL:C], 0)
            dve.memset(attr[:, E_TAIL:C, :], 0.0)
            dve.memset(w_in[:, E_TAIL:C], 0.0).then_inc(cleared, 1)
            dve.memset(onehot[:, G - 2:G, :], 0.0)
            dve.memset(ones[:, :], 1.0)
            dve.wait_ge(iotas, 3)
            dve.tensor_scalar(ident_h[:, :], iota_f[:, :], iota_p[:, 0:1], None, ALU.is_equal)
            dve.tensor_scalar(ident_f[:, :], iota_f[:, :], iota_p[:, 0:1], None, ALU.is_equal)
            dve.tensor_scalar(before[:, :], iota_f[:, :], iota_p[:, 0:1], None, ALU.is_gt)
            dve.tensor_scalar(after[:, :], iota_f[:, :], iota_p[:, 0:1], None, ALU.is_le).then_inc(consts, 1)
            link(dve.tensor_scalar(rank, tmp_i[:, :], float(E), FAR, ALU.is_ge, ALU.mult))
            dve.wait_ge(edges_in, 96)
            for ids_i, to, field in ((src_i, src_t, 0), (dst_i, dst_t, 1)):
                link(dve.tensor_scalar(tmp_i[:, :], ids_i[:, :], 7, None, ALU.logical_shift_right))
                link(dve.tensor_copy(to, tmp_i[:, :]))
                link(dve.tensor_scalar(tmp_i[:, :], ids_i[:, :], P - 1, None, ALU.bitwise_and))
                link(dve.tensor_copy(payload[:, :, field], tmp_i[:, :]))
            dve.memset(key[:, C:C + 1], FAR)
            dve.tensor_copy(payload[:, :, 2], w_in)
            link(dve.scalar_tensor_tensor(out=key[:, 0:C], in0=src_t, scalar=float(T), in1=dst_t,
                                          op0=ALU.mult, op1=ALU.add))
            link(dve.tensor_tensor(key[:, 0:C], key[:, 0:C], rank, ALU.add))
            dve.wait_ge(small_in, 32)
            dve.wait_ge(attrs_in, 32)
            link(dve.tensor_tensor(attr, attr, wedge_b[:, :].unsqueeze(1).to_broadcast([P, C, EDGE_F]), ALU.mult))
            dve.tensor_reduce(third, attr, AX.X, ALU.add).then_inc(gate_sum, 1)
            dve.wait_ge(gates, 1)
            link(dve.tensor_tensor(w_in, src_t, dst_t, ALU.not_equal))
            link(dve.scalar_tensor_tensor(out=third, in0=w_in, scalar=FAR, in1=src_t, op0=ALU.mult, op1=ALU.add))
            dve.tensor_scalar(third, third, float(ROWS2 - 2 * P * T), None, ALU.add).then_inc(payloads, 1)
            dve.wait_ge(payloads, 1)

            def place_steps(h, s):
                group = 2 * h + s
                cols = bass.ds(group * G, G)
                at = PRESET + group * 4

                def step0():
                    dve.wait_ge(rank_read, 2 + G * (group + 1))
                    dve.wait_ge(placed, PRESET + group)
                    dve.tensor_scalar(pos[:, 0, :], rank[:, cols], 3.0 * P, None, ALU.min).then_inc(place_step, 1)

                def step1():
                    dve.wait_ge(place_step, at + 1)
                    dve.scalar_tensor_tensor(out=pos[:, 1, :], in0=pos[:, 0, :], scalar=float(B), in1=key[:, cols],
                                             op0=ALU.mult, op1=ALU.add)
                    dve.scalar_tensor_tensor(out=pos[:, 2, :], in0=pos[:, 0, :], scalar=float(T), in1=third[:, cols],
                                             op0=ALU.mult, op1=ALU.add).then_inc(place_step, 1)

                def step2():
                    dve.wait_ge(place_step, at + 2)
                    dve.tensor_tensor(pos[:, 3, :], pos[:, 2, :], pos[:, 1, :], ALU.subtract).then_inc(place_step, 1)

                def step3():
                    dve.wait_ge(place_step, at + 3)
                    dve.scalar_tensor_tensor(out=pos[:, 2, :], in0=pos[:, 0, :], scalar=2.0 * P, in1=pos[:, 3, :],
                                             op0=ALU.is_ge, op1=ALU.mult).then_inc(place_step, 1)

                def step4():
                    dve.wait_ge(place_step, at + 4)
                    dve.wait_ge(scattered[s], 16 + 16 * G * h)
                    dve.tensor_tensor(place[:, s, :], pos[:, 1, :], pos[:, 2, :], ALU.add).then_inc(placed, 1)

                return [step0, step1, step2, step3, step4]

            dve.sem_inc(place_step, PRESET)
            dve.sem_inc(placed, PRESET)
            dve.memset(junk[:, 0, :], 0.0).then_inc(rank_read, 2)

            def mark(col, v):
                dve.tensor_scalar(onehot[:, v % G, :], iota_b[:, :], key[:, bass.ds(col, 1)], None,
                                  ALU.is_equal).then_inc(oh_ready, 1)

            dve.wait_ge(iotas, 4)
            mark(0, 0)

            def rank_group(group, s, steps):
                for u in range(G):
                    mark(G * group + u + 1, u + 1)
                    dve.wait_ge(rank_ready, G * group + u + 1)
                    a = (G * s + u) % 2
                    dve.scalar_tensor_tensor(out=junk[:, a, :],
                                             in0=counts[a][:, :, :].rearrange("p a b -> p (a b)")[:, 0:B],
                                             scalar=1.0, in1=onehot[:, u, :], op0=ALU.mult, op1=ALU.mult,
                                             accum_out=rank[:, bass.ds(G * group + u, 1)]).then_inc(rank_read, 1)
                    if 0 < u <= len(steps):
                        steps[u - 1]()

            rank_group(0, 0, [])
            with dve.Fori(0, GROUPS // 2 - 1) as it:
                rank_group(2 * it + 1, 1, place_steps(it, 0))
                rank_group(2 * it + 2, 0, place_steps(it, 1))
            rank_group(GROUPS - 1, 1, place_steps(GROUPS // 2 - 1, 0))
            for step in place_steps(GROUPS // 2 - 1, 1):
                step()

            dve.wait_ge(rank_read, 2 + C)
            link(dve.scalar_tensor_tensor(out=third, in0=w_in, scalar=float(P), in1=rank, op0=ALU.mult, op1=ALU.add))
            dve.tensor_scalar(third, third, 3.0 * P, None, ALU.is_ge)
            dve.tensor_scalar(dst_i[:, :], dst_i[:, :], 1, None, ALU.add)
            link(dve.tensor_scalar(src_i[:, :], src_i[:, :], 1, None, ALU.add))
            dve.tensor_tensor(src_i[:, :], src_i[:, :], third, ALU.mult)
            link(dve.tensor_reduce(left_over[:, :], third, AX.X, ALU.add))
            dve.tensor_copy(left_b[:, :], left_over[:, :]).then_inc(left_counted, 1)
            dve.wait_ge(left_summed, 1)
            dve.tensor_copy(left_i[:, :], acc[0][:, 0:1]).then_inc(left_known, 1)

            def layer_input(summed_up=False):
                normed(X[:, :, :], summed_up)
                link(dve.scalar_tensor_tensor(out=H[:, :, :], in0=V[:, :, :], scalar=0.0, in1=rows(stat[:, 3, :]),
                                              op0=ALU.max, op1=ALU.mult))

            dve.wait_ge(oh_ready, C + 1)
            dve.wait_ge(nodes_in, 32)
            layer_input()

            dve.wait_ge(sorted_in, 32)
            for q in range(3):
                if q < 2:
                    plane = slot[:, q * B:(q + 1) * B, :]
                    view = [lambda f, plane=plane: plane[:, :, f].rearrange("p (o t) -> p o t", o=T),
                            lambda f, plane=plane: plane[:, :, f].rearrange("p (t o) -> p o t", o=T)]
                    cols = slice(q, 2 * T, 2)
                else:
                    view = [lambda f: slot[:, 2 * B:CH, f].unsqueeze(2)] * 2
                    cols = slice(2 * T, K)
                for side in (DST, SRC):
                    dve.tensor_copy(near[side][:, :, cols], view[side](side))
                    dve.tensor_copy(far[side][:, :, cols], view[side](1 - side))
                    ins = dve.tensor_copy(wgt[side][:, :, cols], view[side](2 if side == DST else 3))
            link(ins)
            dve.memset(wparts[:, :, :, 0], 1.0)
            for n in plain_msg:
                dve.memset(plain_msg[n][:, :, F], 1.0)
            rest = U[:, :, 0:KP]

            def weight_parts(side):
                return split(wgt[side][:, :, 0:K], lambda n: wparts[:, :, 0:K, n + 1], rest[:, :, 0:K])

            weight_parts(DST).then_inc(wparts_ready, 1)

            def make(side, o, j, g):
                q0, q = FIRST[g] // 4, MSG_QUADS[g]
                for s, ids in enumerate((far[side], near[side])):
                    ins = dve.tensor_tensor(
                        oh[:, j, s, q0:q0 + q, :, :],
                        tile(ids, o)[:, :, 4 * q0:4 * (q0 + q)].rearrange("p a (q c) -> p (a q) c", c=4)
                        .unsqueeze(2).to_broadcast([P, q, P, 4]),
                        iota_4[:, :, :].unsqueeze(1).to_broadcast([P, q, P, 4]), ALU.is_equal)
                ins.then_inc(oh_made, 1)

            dve.wait_ge(iotas, 5)

            def make_counted(o, j, g):
                dve.wait_ge(tiles_full, AHEAD + (o - 2) * NG + g + 1)
                make(DST, o, j, g)

            flow(dve, (0, make_counted))
            dve.wait_ge(deg_read, AHEAD + T)
            dve.wait_ge(tiles_full, AHEAD + NG * T)
            dve.wait_ge(corrected, 1)
            link(dve.tensor_reduce(wsum[:, :], deg[:, :, 1:4], AX.X, ALU.add))
            link(dve.tensor_scalar(dinv[:, 0, :], wsum[:, :], 1.0, None, ALU.add))
            dve.tensor_scalar(stat[:, 1, :], dinv[:, 0, :], 1e-30, None, ALU.max).then_inc(sqrt_in, 1)
            root()
            link(dve.scalar_tensor_tensor(out=dinv[:, 0, :], in0=dinv[:, 0, :], scalar=0.0, in1=stat[:, 3, :],
                                          op0=ALU.is_gt, op1=ALU.mult))
            dve.tensor_scalar(stat[:, 1, :], deg[:, :, 0], 1.0, 1.0, ALU.add, ALU.max).then_inc(sqrt_in, 1)
            root()
            link(dve.tensor_copy(dinv[:, 1, :], stat[:, 3, :]))
            link(dve.tensor_scalar(icnt[:, 0, :], deg[:, :, 0], 1.0, None, ALU.max))
            link(dve.reciprocal(icnt[:, 0, :], icnt[:, 0, :]))
            dve.wait_ge(weights_in, WEIGHTS)
            link(dve.tensor_tensor(bias[:, 1, :], bias[:, 1, :], bias[:, 6, :], ALU.add))

            weighted = counted_layers = 0
            dve.sem_inc(gathered, AHEAD)
            for l in range(5):
                if 0 < l < 4:
                    layer_input(summed_up=l > 1)
                sent = H
                if l < 2:
                    link(dve.tensor_tensor(V[:, :, :], H[:, :, :], rows(dinv[:, l, :]), ALU.mult))
                    sent = V
                dve.sem_inc(sent_ready, 1)
                for h, (lo, hi) in enumerate(HALVES):
                    dve.wait_ge(nodes_high, 2 * l + h + 1)
                    dve.tensor_tensor(U[:, lo:hi, :], sent[:, lo:hi, :], parts[:, lo:hi, 0, :], ALU.subtract).then_inc(nodes_rest, 1)
                for h, (lo, hi) in enumerate(HALVES):
                    dve.wait_ge(nodes_middle, 2 * l + h + 1)
                    ins = dve.tensor_tensor(parts[:, lo:hi, 2, :], U[:, lo:hi, :], parts[:, lo:hi, 1, :], ALU.subtract)
                ins.then_inc(parts_ready, 1)
                if l in WEIGHTED:
                    side = WEIGHTED[l]

                    def make_rows(o, j, g):
                        dve.wait_ge(summed, AHEAD + (weighted * T + o - 2) * NG + g + 1)
                        make(side, o, j, g)

                    def messages(o, j, g):
                        n = (weighted * T + o) * NG + g
                        w = min(K, FIRST[g + 1]) - FIRST[g]
                        dve.wait_ge(gathered, AHEAD + n + 1)
                        dve.wait_ge(summed, AHEAD + n - 3)
                        if g in SPLIT:
                            here = msg[g % 4][:, 0:w * F].rearrange("p (c f) -> p c f", f=F)
                        else:
                            here = plain_msg[g % 4][:, 0:w, 0:F]
                            if l == 2:
                                dve.tensor_copy(plain_msg[g % 4][:, 0:w, F + 1],
                                                tile(wgt[side], o)[:, :, FIRST[g]:FIRST[g] + w].rearrange("p a k -> p (a k)"))
                        dve.tensor_tensor(here,
                                          gat[g % 2][:, 0:w * F].rearrange("p (c f) -> p c f", f=F),
                                          tile(wgt[side], o)[:, :, FIRST[g]:FIRST[g] + w].rearrange("p a k -> p (a k)")
                                          .unsqueeze(2).to_broadcast([P, w, F]), ALU.mult).then_inc(msg_ready, 1)

                    def rest_of(o, j, g):
                        if g in SPLIT:
                            w = min(K, FIRST[g + 1]) - FIRST[g]
                            here = msg[g % 4][:, 0:w * F]
                            dve.wait_ge(high_made, (weighted * T + o) * len(SPLIT) + SPLIT.index(g) + 1)
                            dve.tensor_tensor(here, here, split_msg[:, SPLIT.index(g) % 2, 0, 0:w, :]
                                              .rearrange("p c f -> p (c f)"), ALU.subtract).then_inc(rest_made, 1)

                    def low(o, j, g):
                        if g in SPLIT:
                            w = min(K, FIRST[g + 1]) - FIRST[g]
                            high, middle, low = [split_msg[:, SPLIT.index(g) % 2, n, 0:w, :].rearrange("p c f -> p (c f)")
                                                 for n in range(3)]
                            dve.wait_ge(middle_made, (weighted * T + o) * len(SPLIT) + SPLIT.index(g) + 1)
                            dve.tensor_tensor(low, msg[g % 4][:, 0:w * F], middle, ALU.subtract).then_inc(split_ready, 1)

                    def take(o, j, g):
                        if g == NG - 1:
                            dve.wait_ge(summed, AHEAD + (weighted * T + o + 1) * NG)
                            if l == 2:
                                dve.tensor_copy(tile(agg, o)[:, :, F:F + 6].rearrange("p a f -> p (a f)"),
                                                acc[j][:, 4 * F:4 * F + 6])
                            dve.tensor_reduce(tile(agg, o)[:, :, 0:F].rearrange("p a f -> p (a f)"),
                                              acc[j][:, 0:4 * F].rearrange("p (x f) -> p f x", x=4),
                                              AX.X, ALU.add).then_inc(agg_ready, 1)

                    flow(dve, (0, make_rows), (5, rest_of), (4, messages), (6, low), (8, take))
                    weighted += 1
                    dve.wait_ge(agg_ready, AHEAD + weighted * T)
                else:
                    if l == 1:
                        weight_parts(SRC).then_inc(wparts_ready, 1)
                    with dve.Fori(0, T // RING) as it:
                        for r in range(RING):
                            m = counted_layers * T + RING * it + r
                            dve.wait_ge(counted, AHEAD + m + 1)
                            dve.tensor_reduce(tile(agg, RING * it + r)[:, :, 0:F].rearrange("p a f -> p (a f)"),
                                              acc[r % 2][:, 0:3 * F].rearrange("p (x f) -> p f x", x=3),
                                              AX.X, ALU.add).then_inc(counts_read, 1)
                    counted_layers += 1
                    dve.wait_ge(counts_read, AHEAD + counted_layers * T)
                dve.wait_ge(corrected, l + 2)
                if l == 2:
                    link(dve.tensor_reduce(gsum[:, :], agg[:, :, F + 3:F + 6], AX.X, ALU.add))
                    dve.tensor_tensor(gsum[:, :], gsum[:, :], agg[:, :, F + 1], ALU.add)
                    link(dve.tensor_tensor(icnt[:, 1, :], agg[:, :, F], agg[:, :, F + 2], ALU.add))
                    link(dve.tensor_scalar(icnt[:, 1, :], icnt[:, 1, :], 1.0, None, ALU.max))
                    link(dve.reciprocal(icnt[:, 1, :], icnt[:, 1, :]))
                    link(dve.tensor_tensor(TH[:, :, F], gsum[:, :], icnt[:, 1, :], ALU.mult))
                for q in range(NQ):
                    a, b = 4 * q, min(T, 4 * q + 4)
                    if l < 2:
                        link(dve.tensor_tensor(U[:, a:b, :], agg[:, a:b, 0:F], V[:, a:b, :], ALU.add))
                        sums, scale = U[:, a:b, :], dinv[:, l, a:b]
                    else:
                        sums, scale = agg[:, a:b, 0:F], icnt[:, 1 if l == 2 else 0, a:b]
                    dve.tensor_tensor(TH[:, a:b, 0:F], sums, rows(scale), ALU.mult).then_inc(th_ready, 1)
                for q in range(NQ):
                    n = NQ * l + q
                    a, b = 4 * q, min(T, 4 * q + 4)
                    dve.wait_ge(projected, n + 1)
                    came = proj[n % 2][:, 0:(b - a) * F].rearrange("p (t f) -> p t f", f=F)
                    if l == 2:
                        dve.tensor_tensor(X[:, a:b, :], X[:, a:b, :], came, ALU.add).then_inc(proj_read, 1)
                    else:
                        dve.tensor_tensor(U[:, a:b, :], came,
                                          bias[:, {0: 0, 1: 1, 3: 2, 4: 3}[l], :].unsqueeze(1).to_broadcast([P, b - a, F]),
                                          ALU.add).then_inc(proj_read, 1)
                    dve.wait_ge(proj_read, n + 1)
                    if l == 0:
                        ins = dve.tensor_reduce(stat[:, 0, a:b], U[:, a:b, :], AX.X, ALU.add)
                    elif l == 3:
                        ins = dve.tensor_scalar(H[:, a:b, :], U[:, a:b, :], 0.0, None, ALU.max)
                    elif l == 4:
                        dve.tensor_tensor(X[:, a:b, :], X[:, a:b, :], U[:, a:b, :], ALU.add).then_inc(result, 1)
                    else:
                        if l == 1:
                            link(dve.tensor_tensor(X[:, a:b, :], X[:, a:b, :], U[:, a:b, :], ALU.add))
                        ins = dve.tensor_reduce(stat[:, 0, a:b], X[:, a:b, :], AX.X, ALU.add)
                if l < 4:
                    link(ins)
                if l == 0:
                    normed(U[:, :, :], summed_up=True)
                    link(dve.tensor_tensor(V[:, :, :], V[:, :, :], rows(stat[:, 3, :]), ALU.mult))
                    link(dve.tensor_tensor(V[:, :, :], V[:, :, :], bias[:, 4, :].unsqueeze(1).to_broadcast([P, T, F]), ALU.mult))
                    dve.tensor_tensor(V[:, :, :], V[:, :, :], bias[:, 5, :].unsqueeze(1).to_broadcast([P, T, F]),
                                      ALU.add).then_inc(gelu_in, 1)
                    dve.wait_ge(gelu_out, 1)
                    link(dve.tensor_tensor(X[:, :, :], X[:, :, :], U[:, :, :], ALU.add))

        @block.tensor
        def _(pe):
            pe.sem_inc(tiles_full, AHEAD)
            pe.sem_inc(tiles_read, AHEAD)
            pe.sem_inc(deg_read, AHEAD)
            pe.sem_inc(agg_ready, AHEAD)
            pe.sem_inc(summed, AHEAD)
            pe.sem_inc(gat_ready, AHEAD)
            pe.sem_inc(msg_ready, AHEAD)
            pe.sem_inc(counted, AHEAD)
            pe.sem_inc(counts_read, AHEAD)
            pe.wait_ge(consts, 1)
            for a in range(2):
                for lo, hi in ((0, 512), (512, B)):
                    pe.matmul(counts[a][:, lo // 512, 0:hi - lo], ones[:, :], onehot[:, G - 1, lo:hi], start=True, stop=True,
                              skip_group_check=True)

            def count(a, left, v):
                for lo, hi in ((0, 512), (512, B)):
                    ins = pe.matmul(counts[a][:, lo // 512, 0:hi - lo], left[:, :], onehot[:, v % G, lo:hi],
                                    start=False, stop=True, skip_group_check=True)
                return ins

            with pe.Fori(0, GROUPS // 2) as it:
                for v in range(2 * G):
                    pe.wait_ge(rank_read, 2 * G * it + v + 1)
                    count(v % 2, after, v - 2)
                    count(v % 2, ones, v - 1)
                    pe.wait_ge(oh_ready, 2 * G * it + v + 1)
                    count(v % 2, before, v).then_inc(rank_ready, 1)

            pe.wait_ge(left_counted, 1)
            pe.matmul(acc[0][:, 0:1], ones[:, :], left_b[:, :], start=True, stop=True).then_inc(left_summed, 1)
            pe.wait_ge(weights_in, WEIGHTS)
            pe.transpose(acc[1][0:F, 0:F], wn[:, :], ident_f[0:F, 0:F]).then_inc(wn_turned, 1)
            pe.wait_ge(wn_ready, 1)
            pe.wait_ge(wparts_ready, 1)

            def count_tiles(o, j, g):
                n = o * NG + g
                pe.wait_ge(oh_made, n + 1)
                pe.wait_ge(tiles_read, AHEAD + n - 1)
                if g == 0:
                    pe.wait_ge(deg_read, AHEAD + o - 1)
                for k in range(FIRST[g], min(K, FIRST[g + 1])):
                    t = k // 2 - FIRST[g] // 2
                    rows_n = oh[:, j, 1, k // 4, :, k % 4]
                    pe.matmul(tiles[g % 2][:, t * P:(t + 1) * P], oh[:, j, 0, k // 4, :, k % 4], rows_n,
                              start=(k % 2 == 0), stop=(k % 2 == 1 or k == K - 1))
                    ins = pe.matmul(acc[j][:, 0:4], rows_n, tile(wparts, o)[:, :, k, :].rearrange("p a w -> p (a w)"),
                                    start=(k == 0), stop=(k == K - 1))
                ins.then_inc(tiles_full, 1)

            flow(pe, (0, count_tiles))

            weighted = counted_layers = 0
            for l in range(5):
                pe.wait_ge(parts_ready, l + 1)
                if l in WEIGHTED:
                    side = WEIGHTED[l]
                    pe.wait_ge(wparts_ready, weighted + 1)

                    def turn_oh(o, j, g):
                        n = (weighted * T + o) * NG + g
                        pe.wait_ge(oh_made, T * NG + n + 1)
                        pe.wait_ge(gat_ready, AHEAD + n - 1)
                        for k in range(FIRST[g], min(K, FIRST[g + 1])):
                            c = k - FIRST[g]
                            ins = pe.transpose(turned_oh[g % 2][:, c * P:(c + 1) * P], oh[:, j, 0, k // 4, :, k % 4], ident_h[:, :])
                        ins.then_inc(oh_turned, 1)

                    def gather(o, j, g):
                        n = (weighted * T + o) * NG + g
                        pe.wait_ge(gat_ready, AHEAD + n + 1)
                        pe.wait_ge(msg_ready, AHEAD + n - 1)
                        for k in range(FIRST[g], min(K, FIRST[g + 1])):
                            c = k - FIRST[g]
                            for part in range(3):
                                here = parts[:, k // 2, part, :] if k < 2 * T else tile(parts, o)[:, :, part, :].rearrange("p a f -> p (a f)")
                                ins = pe.matmul(gat[g % 2][:, c * F:(c + 1) * F], gat_t[:, g % 2, c * P:(c + 1) * P], here,
                                                start=(part == 0), stop=(part == 2))
                        ins.then_inc(gathered, 1)

                    def sum_up(o, j, g):
                        n = (weighted * T + o) * NG + g
                        if g in SPLIT:
                            pe.wait_ge(split_ready, (weighted * T + o) * len(SPLIT) + SPLIT.index(g) + 1)
                        else:
                            pe.wait_ge(msg_ready, AHEAD + n + 1)
                            pe.wait_ge(sum_ready, (weighted * T + o) * len(PLAIN) + PLAIN.index(g) + 1)
                        if g == 0:
                            pe.wait_ge(agg_ready, AHEAD + weighted * T + o - 1)
                        for k in range(FIRST[g], min(K, FIRST[g + 1])):
                            c = k - FIRST[g]
                            if g in SPLIT:
                                ins = pe.matmul(acc[j][:, 0:3 * F], oh[:, j, 1, k // 4, :, k % 4],
                                                split_msg[:, SPLIT.index(g) % 2, :, c, :],
                                                start=False, stop=(k == K - 1), skip_group_check=True)
                            else:
                                width = F if l == 0 else PW
                                ins = pe.matmul(acc[j][:, 3 * F:3 * F + width],
                                                sum_f[:, PLAIN.index(g) % 2, c * P:(c + 1) * P],
                                                plain_msg[g % 4][:, c, 0:width],
                                                start=(k == 0), stop=False, skip_group_check=True)
                            if l == 2 and g in SPLIT:
                                ins = pe.matmul(acc[j][:, 3 * F + PW:3 * F + PW + 4], oh[:, j, 1, k // 4, :, k % 4],
                                                tile(wparts, o)[:, :, k, :].rearrange("p a w -> p (a w)"),
                                                start=False, stop=(k == K - 1), skip_group_check=True)
                        ins.then_inc(summed, 1)

                    flow(pe, (2, turn_oh), (3, gather), (7, sum_up))
                    weighted += 1
                else:
                    with pe.Fori(0, T // RING) as it:
                        for r in range(RING):
                            o = RING * it + r
                            m = counted_layers * T + o
                            pe.wait_ge(counts_in[r], 16 * (counted_layers * (T // RING) + it + 1))
                            pe.wait_ge(counts_read, AHEAD + (m - 1 if r else m))
                            for t in range(TC):
                                here = (parts[:, t, :, :] if t < T else tile(parts, o).rearrange("p a x f -> p (a x) f"))
                                ins = pe.matmul(acc[r % 2][:, 0:3 * F], cnt_in[:, r, t * P:(t + 1) * P],
                                                here.rearrange("p x f -> p (x f)"), start=(t == 0), stop=(t == TC - 1))
                            ins.then_inc(counted, 1)
                    counted_layers += 1

                def turns(q):
                    n = NQ * l + q
                    pe.wait_ge(th_ready, n + 1)
                    if n >= 2:
                        pe.wait_ge(tht_ready, n - 1)
                    for t in range(4 * q, min(T, 4 * q + 4)):
                        ins = pe.transpose(turn[n % 2][:, t % 4 * P:(t % 4 + 1) * P], TH[:, t, :], ident_f[:, :])
                    ins.then_inc(turned, 1)

                turns(0)
                for q in range(NQ):
                    n = NQ * l + q
                    if q + 1 < NQ:
                        turns(q + 1)
                    pe.wait_ge(tht_ready, n + 1)
                    if n >= 2:
                        pe.wait_ge(proj_read, n - 1)
                    for t in range(4 * q, min(T, 4 * q + 4)):
                        ins = pe.matmul(proj[n % 2][:, t % 4 * F:(t % 4 + 1) * F], tht[:, n % 2, t % 4 * P:(t % 4 + 1) * P],
                                        WS[:, l, :], start=True, stop=True)
                    ins.then_inc(projected, 1)


_INS = ["x", "src", "dst", "edge_attr_16", "edge_weight1", "L0_gnn_W", "L0_gnn_b", "L0_gnn_gamma", "L0_gnn_beta",
        "L1_gnn_W", "L1_gnn_b", "L1_gnn_W_lin", "L1_gnn_b_lin", "L2_gnn_W_edge", "L2_gnn_b_edge", "L2_gnn_W_node",
        "L2_gnn_b_node", "L3_gnn_w1_l", "L3_gnn_b1", "L3_gnn_w1_r", "L3_gnn_w2_l", "L3_gnn_b2", "L3_gnn_w2_r"]


def kernel(**inputs):
    import numpy as _np
    import concourse.bacc as _bacc
    from concourse.bass_utils import run_bass_kernel_spmd as _run

    nc = _bacc.Bacc("TRN2", target_bir_lowering=False, num_devices=1)
    arrays, args = {}, []
    for name in _INS:
        a = _np.ascontiguousarray(inputs[name])
        arrays[f"in_{name}"] = a
        args.append(nc.dram_tensor(f"in_{name}", a.shape, mybir.dt.from_np(a.dtype), kind="ExternalInput").ap())
    args.append(nc.dram_tensor("out", (N, F), f32, kind="ExternalOutput").ap())
    args.append(nc.dram_tensor("slots", (ROWS, 4), f32).ap())
    args.append(nc.dram_tensor("count_table", (T, P, TC * P), bf16).ap())
    args.append(nc.dram_tensor("rows_table", (T * P + 1, F), f32).ap())
    args.append(nc.dram_tensor("added_table", (T * P + 1, F + 2), f32).ap())
    args.append(nc.dram_tensor("marks_table", (2, P, C), i32).ap())
    args.append(nc.dram_tensor("fields_table", (P * C, 4), f32).ap())
    gnn(nc, *args)
    return _run(nc, [arrays], core_ids=[0]).results[0]["out"]
```
